# Optimizing a Trainium2 kernel written in Bass

```python
import numpy as np
import jax
import jax.numpy as jnp

def _softmax(x, axis=-1):
    return jax.nn.softmax(x, axis=axis)

def _gelu(x):
    return jax.nn.gelu(x, approximate=True)

def _silu(x):
    return jax.nn.silu(x)

def _sigmoid(x):
    return jax.nn.sigmoid(x)

def _layernorm(x, axis=-1, eps=1e-05):
    m = jnp.mean(x, axis=axis, keepdims=True)
    v = jnp.var(x, axis=axis, keepdims=True)
    return (x - m) / jnp.sqrt(v + eps)

def _scatter_add(tgt, idx, src, axis=0):
    return tgt.at[idx].add(src)

def _segment_sum(src, seg, n):
    return jax.ops.segment_sum(src, seg, n)
kernel_name = 'mk_seq_preln_d1_jaxref_r8_c805de'

def setup_inputs(seed: int=0):
    np.random.seed(seed)
    _w = jnp.asarray

    def _L0_attn_setup():
        import jax, jax.numpy as jnp
        import numpy as np
        B, T, C, F = (8, 256, 128, 512)

        def _ln(x, g, b):
            m = jnp.mean(x, axis=-1, keepdims=True)
            v = jnp.mean((x - m) ** 2, axis=-1, keepdims=True)
            return (x - m) * jax.lax.rsqrt(v + 1e-05) * g + b

        def _shift(x):
            return jnp.pad(x, ((0, 0), (1, 0), (0, 0)))[:, :-1]

        def _wkv(w, u, k, v):
            kT = jnp.swapaxes(k, 0, 1)
            vT = jnp.swapaxes(v, 0, 1)
            b, c = (k.shape[0], k.shape[2])
            aa = jnp.zeros((b, c), k.dtype)
            bb = jnp.zeros((b, c), k.dtype)
            pp = jnp.full((b, c), -1e+38, k.dtype)

            def step(carry, kv_t):
                aa, bb, pp = carry
                kt, vt = kv_t
                ww = u + kt
                p = jnp.maximum(pp, ww)
                e1 = jnp.exp(pp - p)
                e2 = jnp.exp(ww - p)
                out = (e1 * aa + e2 * vt) / (e1 * bb + e2)
                ww2 = pp + w
                p2 = jnp.maximum(ww2, kt)
                e1 = jnp.exp(ww2 - p2)
                e2 = jnp.exp(kt - p2)
                return ((e1 * aa + e2 * vt, e1 * bb + e2, p2), out)
            _, outs = jax.lax.scan(step, (aa, bb, pp), (kT, vT))
            return jnp.swapaxes(outs, 0, 1)
        key = jax.random.key(seed)
        ks = jax.random.split(key, 16)
        s = 1.0 / np.sqrt(C)
        inp = {'x': jax.random.normal(ks[0], (B, T, C), jnp.float32), 'ln0_g': jnp.ones((C,), jnp.float32), 'ln0_b': jnp.zeros((C,), jnp.float32), 'ln1_g': jnp.ones((C,), jnp.float32), 'ln1_b': jnp.zeros((C,), jnp.float32), 'time_decay': jax.random.normal(ks[1], (C,), jnp.float32) * 0.5, 'time_first': jax.random.normal(ks[2], (C,), jnp.float32) * 0.5, 'tm_k': jax.random.uniform(ks[3], (C,), jnp.float32), 'tm_v': jax.random.uniform(ks[4], (C,), jnp.float32), 'tm_r': jax.random.uniform(ks[5], (C,), jnp.float32), 'Wk': jax.random.normal(ks[6], (C, C), jnp.float32) * s, 'Wv': jax.random.normal(ks[7], (C, C), jnp.float32) * s, 'Wr': jax.random.normal(ks[8], (C, C), jnp.float32) * s, 'Wo': jax.random.normal(ks[9], (C, C), jnp.float32) * s, 'cm_k': jax.random.uniform(ks[10], (C,), jnp.float32), 'cm_r': jax.random.uniform(ks[11], (C,), jnp.float32), 'Wck': jax.random.normal(ks[12], (C, F), jnp.float32) * s, 'Wcv': jax.random.normal(ks[13], (F, C), jnp.float32) * (1.0 / np.sqrt(F)), 'Wcr': jax.random.normal(ks[14], (C, C), jnp.float32) * s}
        return inp
    _L0_attn_in = _L0_attn_setup()

    def _L0_ffn_setup():
        import jax, jax.numpy as jnp
        import numpy as np
        B, S, D, H, E, F, K = (2, 128, 128, 16, 8, 512, 2)
        EPS = 1e-05

        def _layernorm(x, g, b):
            mu = jnp.mean(x, axis=-1, keepdims=True)
            var = jnp.mean(jnp.square(x - mu), axis=-1, keepdims=True)
            return (x - mu) * jax.lax.rsqrt(var + EPS) * g + b
        key = jax.random.key(seed)
        ks = jax.random.split(key, 12)
        w = lambda k, shape: jax.random.normal(k, shape, dtype=jnp.float32) * 0.02
        return {'x': jax.random.normal(ks[0], (B, S, D), dtype=jnp.float32), 'ln1_g': jnp.ones((D,), jnp.float32), 'ln1_b': jnp.zeros((D,), jnp.float32), 'ln2_g': jnp.ones((D,), jnp.float32), 'ln2_b': jnp.zeros((D,), jnp.float32), 'Wq': w(ks[1], (D, D)), 'Wk': w(ks[2], (D, D)), 'Wv': w(ks[3], (D, D)), 'Wo': w(ks[4], (D, D)), 'Wg': w(ks[5], (D, E)), 'W1': w(ks[6], (E, D, F)), 'b1': jnp.zeros((E, F), jnp.float32), 'W2': w(ks[7], (E, F, D)), 'b2': jnp.zeros((E, D), jnp.float32)}
    _L0_ffn_in = _L0_ffn_setup()
    _d = {'L0_attn_x': _L0_attn_in['x'], 'L0_attn_ln0_g': _L0_attn_in['ln0_g'], 'L0_attn_ln0_b': _L0_attn_in['ln0_b'], 'L0_attn_ln1_g': _L0_attn_in['ln1_g'], 'L0_attn_ln1_b': _L0_attn_in['ln1_b'], 'L0_attn_time_decay': _L0_attn_in['time_decay'], 'L0_attn_time_first': _L0_attn_in['time_first'], 'L0_attn_tm_k': _L0_attn_in['tm_k'], 'L0_attn_tm_v': _L0_attn_in['tm_v'], 'L0_attn_tm_r': _L0_attn_in['tm_r'], 'L0_attn_Wk': _L0_attn_in['Wk'], 'L0_attn_Wv': _L0_attn_in['Wv'], 'L0_attn_Wr': _L0_attn_in['Wr'], 'L0_attn_Wo': _L0_attn_in['Wo'], 'L0_attn_cm_k': _L0_attn_in['cm_k'], 'L0_attn_cm_r': _L0_attn_in['cm_r'], 'L0_attn_Wck': _L0_attn_in['Wck'], 'L0_attn_Wcv': _L0_attn_in['Wcv'], 'L0_attn_Wcr': _L0_attn_in['Wcr'], 'L0_ffn_ln1_g': _L0_ffn_in['ln1_g'], 'L0_ffn_ln1_b': _L0_ffn_in['ln1_b'], 'L0_ffn_ln2_g': _L0_ffn_in['ln2_g'], 'L0_ffn_ln2_b': _L0_ffn_in['ln2_b'], 'L0_ffn_Wq': _L0_ffn_in['Wq'], 'L0_ffn_Wk': _L0_ffn_in['Wk'], 'L0_ffn_Wv': _L0_ffn_in['Wv'], 'L0_ffn_Wo': _L0_ffn_in['Wo'], 'L0_ffn_Wg': _L0_ffn_in['Wg'], 'L0_ffn_W1': _L0_ffn_in['W1'], 'L0_ffn_b1': _L0_ffn_in['b1'], 'L0_ffn_W2': _L0_ffn_in['W2'], 'L0_ffn_b2': _L0_ffn_in['b2']}
    _x0 = _d['L0_attn_x']
    _d['L0_attn_x'] = jax.random.normal(jax.random.fold_in(jax.random.key(seed), 1), (8, 512, 128), dtype=_x0.dtype)
    del _x0
    return _d

def reference(L0_attn_x, L0_attn_ln0_g, L0_attn_ln0_b, L0_attn_ln1_g, L0_attn_ln1_b, L0_attn_time_decay, L0_attn_time_first, L0_attn_tm_k, L0_attn_tm_v, L0_attn_tm_r, L0_attn_Wk, L0_attn_Wv, L0_attn_Wr, L0_attn_Wo, L0_attn_cm_k, L0_attn_cm_r, L0_attn_Wck, L0_attn_Wcv, L0_attn_Wcr, L0_ffn_ln1_g, L0_ffn_ln1_b, L0_ffn_ln2_g, L0_ffn_ln2_b, L0_ffn_Wq, L0_ffn_Wk, L0_ffn_Wv, L0_ffn_Wo, L0_ffn_Wg, L0_ffn_W1, L0_ffn_b1, L0_ffn_W2, L0_ffn_b2):

    def _L0_attn_ref(x, ln0_g, ln0_b, ln1_g, ln1_b, time_decay, time_first, tm_k, tm_v, tm_r, Wk, Wv, Wr, Wo, cm_k, cm_r, Wck, Wcv, Wcr):
        import jax, jax.numpy as jnp
        import numpy as np
        B, T, C, F = (8, 256, 128, 512)

        def _ln(x, g, b):
            m = jnp.mean(x, axis=-1, keepdims=True)
            v = jnp.mean((x - m) ** 2, axis=-1, keepdims=True)
            return (x - m) * jax.lax.rsqrt(v + 1e-05) * g + b

        def _shift(x):
            return jnp.pad(x, ((0, 0), (1, 0), (0, 0)))[:, :-1]

        def _wkv(w, u, k, v):
            kT = jnp.swapaxes(k, 0, 1)
            vT = jnp.swapaxes(v, 0, 1)
            b, c = (k.shape[0], k.shape[2])
            aa = jnp.zeros((b, c), k.dtype)
            bb = jnp.zeros((b, c), k.dtype)
            pp = jnp.full((b, c), -1e+38, k.dtype)

            def step(carry, kv_t):
                aa, bb, pp = carry
                kt, vt = kv_t
                ww = u + kt
                p = jnp.maximum(pp, ww)
                e1 = jnp.exp(pp - p)
                e2 = jnp.exp(ww - p)
                out = (e1 * aa + e2 * vt) / (e1 * bb + e2)
                ww2 = pp + w
                p2 = jnp.maximum(ww2, kt)
                e1 = jnp.exp(ww2 - p2)
                e2 = jnp.exp(kt - p2)
                return ((e1 * aa + e2 * vt, e1 * bb + e2, p2), out)
            _, outs = jax.lax.scan(step, (aa, bb, pp), (kT, vT))
            return jnp.swapaxes(outs, 0, 1)
        xa = _ln(x, ln0_g, ln0_b)
        xs = _shift(xa)
        k = (xa * tm_k + xs * (1.0 - tm_k)) @ Wk
        v = (xa * tm_v + xs * (1.0 - tm_v)) @ Wv
        r = jax.nn.sigmoid((xa * tm_r + xs * (1.0 - tm_r)) @ Wr)
        w = -jnp.exp(time_decay)
        wkv = _wkv(w, time_first, k, v)
        x = x + r * wkv @ Wo
        xc = _ln(x, ln1_g, ln1_b)
        xs = _shift(xc)
        kk = (xc * cm_k + xs * (1.0 - cm_k)) @ Wck
        kv = jnp.square(jax.nn.relu(kk)) @ Wcv
        rr = jax.nn.sigmoid((xc * cm_r + xs * (1.0 - cm_r)) @ Wcr)
        return x + rr * kv

    def _L0_ffn_ref(x, ln1_g, ln1_b, ln2_g, ln2_b, Wq, Wk, Wv, Wo, Wg, W1, b1, W2, b2):
        import jax, jax.numpy as jnp
        import numpy as np
        B, S, D, H, E, F, K = (2, 128, 128, 16, 8, 512, 2)
        EPS = 1e-05

        def _layernorm(x, g, b):
            mu = jnp.mean(x, axis=-1, keepdims=True)
            var = jnp.mean(jnp.square(x - mu), axis=-1, keepdims=True)
            return (x - mu) * jax.lax.rsqrt(var + EPS) * g + b
        Bb, Ss, Dd = x.shape
        Dh = Dd // H
        h = _layernorm(x, ln1_g, ln1_b)
        q = (h @ Wq).reshape(Bb, Ss, H, Dh)
        k = (h @ Wk).reshape(Bb, Ss, H, Dh)
        v = (h @ Wv).reshape(Bb, Ss, H, Dh)
        scores = jnp.einsum('bqhd,bkhd->bhqk', q, k) / jnp.sqrt(jnp.float32(Dh))
        attn = jax.nn.softmax(scores, axis=-1)
        ctx = jnp.einsum('bhqk,bkhd->bqhd', attn, v).reshape(Bb, Ss, Dd)
        x = x + ctx @ Wo
        m = _layernorm(x, ln2_g, ln2_b)
        xt = m.reshape(-1, Dd)
        T = xt.shape[0]
        probs = jax.nn.softmax(xt @ Wg, axis=-1)
        wts, idx = jax.lax.top_k(probs, K)
        wts = wts / jnp.sum(wts, axis=-1, keepdims=True)
        h1 = jax.nn.gelu(jnp.einsum('td,edf->etf', xt, W1) + b1[:, None, :])
        ye = jnp.einsum('etf,efd->etd', h1, W2) + b2[:, None, :]
        sel = ye[idx, jnp.arange(T)[:, None], :]
        moe_out = jnp.sum(wts[..., None] * sel, axis=1).reshape(Bb, Ss, Dd)
        return x + moe_out
    x = L0_attn_x
    x = x + _L0_attn_ref(_layernorm(x, axis=-1), L0_attn_ln0_g, L0_attn_ln0_b, L0_attn_ln1_g, L0_attn_ln1_b, L0_attn_time_decay, L0_attn_time_first, L0_attn_tm_k, L0_attn_tm_v, L0_attn_tm_r, L0_attn_Wk, L0_attn_Wv, L0_attn_Wr, L0_attn_Wo, L0_attn_cm_k, L0_attn_cm_r, L0_attn_Wck, L0_attn_Wcv, L0_attn_Wcr)
    x = x + _L0_ffn_ref(_layernorm(x, axis=-1), L0_ffn_ln1_g, L0_ffn_ln1_b, L0_ffn_ln2_g, L0_ffn_ln2_b, L0_ffn_Wq, L0_ffn_Wk, L0_ffn_Wv, L0_ffn_Wo, L0_ffn_Wg, L0_ffn_W1, L0_ffn_b1, L0_ffn_W2, L0_ffn_b2)
    return x

_drawn_inputs = setup_inputs


def setup_inputs(seed=0):
    import zlib

    import numpy as np

    out = dict(_drawn_inputs(seed))
    spreads = {'L0_attn_ln0_g': (1.0, 0.2),
     'L0_attn_ln0_b': (0.0, 0.1),
     'L0_attn_ln1_g': (1.0, 0.2),
     'L0_attn_ln1_b': (0.0, 0.1),
     'L0_ffn_ln1_g': (1.0, 0.6),
     'L0_ffn_ln1_b': (0.0, 0.8),
     'L0_ffn_ln2_g': (1.0, 0.6),
     'L0_ffn_ln2_b': (0.0, 0.8),
     'L0_ffn_b1': (0.0, 0.8),
     'L0_ffn_b2': (0.0, 0.357)}
    factors = {'L0_ffn_Wq': 8.0,
     'L0_ffn_Wk': 8.0,
     'L0_ffn_Wv': 8.0,
     'L0_ffn_Wo': 8.0,
     'L0_ffn_W1': 4.485,
     'L0_ffn_W2': 4.038}
    for name, (base, spread) in spreads.items():
        noise = np.random.default_rng([zlib.crc32(name.encode()), seed]).standard_normal(out[name].shape)
        drawn = base * np.exp(spread * noise) if base else spread * noise
        out[name] = jnp.asarray(drawn.astype(out[name].dtype))
    for name, factor in factors.items():
        out[name] = (out[name] * factor).astype(out[name].dtype)
    return out
```

```python
from contextlib import ExitStack

import concourse.bass as bass
from concourse import mybir

F32 = mybir.dt.float32
F32R = mybir.dt.float32r
U32 = mybir.dt.uint32
ALU = mybir.AluOpType
ACT = mybir.ActivationFunctionType
AX_X = mybir.AxisListType.X

P = 128
EPS = 1e-5
VEC = ["L0_attn_ln0_g", "L0_attn_ln0_b", "L0_attn_ln1_g", "L0_attn_ln1_b", "L0_attn_time_decay",
       "L0_attn_time_first", "L0_attn_tm_k", "L0_attn_tm_v", "L0_attn_tm_r", "L0_attn_cm_k",
       "L0_attn_cm_r", "L0_ffn_ln1_g", "L0_ffn_ln1_b", "L0_ffn_ln2_g", "L0_ffn_ln2_b"]
SQUARE = ["L0_attn_Wk", "L0_attn_Wv", "L0_attn_Wr", "L0_attn_Wo", "L0_attn_Wcr",
          "L0_ffn_Wq", "L0_ffn_Wk", "L0_ffn_Wv", "L0_ffn_Wo"]


class Signal:

    def __init__(self, handle, per):
        self.sem, self.per = handle, per

    def at(self, b, k):
        return b * self.per + k


def after(engine, signal, b, k):
    value = signal.at(b, k)
    if not isinstance(value, int) or value > 0:
        engine.wait_ge(signal.sem, value)


class Chain:

    def __init__(self, engine, handle, per):
        self.engine, self.sem, self.per = engine, handle, per

    def begin(self, b):
        self.b, self.k = b, 0

    def step(self, instruction):
        self.k += 1
        instruction.then_inc(self.sem, 1)

    def wait(self):
        self.engine.wait_ge(self.sem, self.b * self.per + self.k)

    def link(self, instruction):
        self.step(instruction)
        self.wait()

    def end(self):
        assert self.k == self.per, (self.sem, self.k, self.per)


def build(nc, t, out):
    x = t["L0_attn_x"]
    B, T, C = x.shape
    NT = T // P
    F = t["L0_attn_Wck"].shape[1]
    NF = F // P
    E = t["L0_ffn_Wg"].shape[1]
    H, DH = 16, C // 16
    G = 4
    NG = H // G
    HW = P // G
    RS = 3 * DH
    RM = RS + 2
    SCALE = float(DH) ** -0.5
    NEG = -1e38
    assert C == P and T == 512 and E == 8 and NF == 4

    with ExitStack() as ctx:
        def sb(name, shape, dt=F32):
            return ctx.enter_context(nc.sbuf_tensor(name, shape, dt))

        def bank(name, shape):
            return ctx.enter_context(nc.psum_tensor(name, shape, F32))

        def sig(name, per=1):
            return Signal(ctx.enter_context(nc.semaphore(name)), per)

        def sem(name):
            return ctx.enter_context(nc.semaphore(name))

        sq = {n: sb(n, [P, C]) for n in SQUARE}
        wck = sb("wck", [P, F])
        wcv = sb("wcv", [P, NF, C])
        wg = sb("wg", [P, E])
        b2 = sb("b2", [E, C])
        w1h = sb("w1h", [P, E, F], F32R)
        w1l = sb("w1l", [P, E, F], F32R)
        w2 = sb("w2", [P, E, NF, C])
        NV = len(VEC)
        rows = sb("rows", [NV + E * NF, P])
        cols = sb("cols", [P, NV + E * NF])
        ident = sb("ident", [P, P])
        half = sb("half", [P, NT])
        iota = sb("iota", [P, E])
        idle = sb("idle", [P, 16])
        idle_turn = [0]
        wdec = sb("wdec", [P, 1])
        wrow = sb("wrow", [P, T])
        col = {n: cols[:, i:i + 1] for i, n in enumerate(VEC)}

        X = sb("X", [P, NT, C])
        Z0 = sb("Z0", [P, NT, C])
        ZA = sb("ZA", [P, NT, C])
        XA = sb("XA", [P, T + 1])
        D = sb("D", [P, T])
        MK = sb("MK", [P, T])
        MV = sb("MV", [P, T])
        MR = sb("MR", [P, T])
        K = sb("K", [P, T])
        V = sb("V", [P, T])
        R = sb("R", [P, T])
        PP = sb("PP", [P, T + 1])
        EE = sb("EE", [P, 4, T])
        EV = sb("EV", [P, T])
        AA = sb("AA", [P, T + 1])
        BB = sb("BB", [P, T + 1])
        N1 = sb("N1", [P, T])
        N2 = K
        D1 = D
        DD = EV
        GT = MV
        Y1 = sb("Y1", [P, NT, C])
        KK = EE
        RT = Z0
        X1 = sb("X1", [P, NT, C])
        Z1 = sb("Z1", [P, NT, C])
        HT = MK
        QA = sb("QA", [P, NT, H, HW])
        KA = sb("KA", [P, NT, H, HW])
        VA = sb("VA", [P, NT, H, HW])
        KT = sb("KT", [P, NG, T], F32R)
        Q1 = sb("Q1", [P, NG, T], F32R)
        stA = sb("stA", [P, NT, 6])
        mvA = sb("mvA", [P, NT, 2])
        rsA = sb("rsA", [P, 4, NT])

        NM = sb("NM", [P, NT, H])
        Q2 = sb("Q2", [P, 2, T], F32R)
        PT = sb("PT", [P, 2 * G, T])
        CT = sb("CT", [P, T])
        RD = sb("RD", [P, NT, G])
        CX = sb("CX", [P, NT, H, DH])
        Z1b = sb("Z1b", [P, NT, C])

        CXT = sb("CXT", [P, T])
        Y3 = sb("Y3", [P, NT, C])
        XZ = sb("XZ", [P, NT, C])
        RES = sb("RES", [P, NT, C])
        ZM = sb("ZM", [P, NT, C])
        MT = sb("MT", [P, T])
        MH = sb("MH", [P, T], F32R)
        ML = sb("ML", [P, T], F32R)
        H1 = sb("H1", [P, 2, NF, T])
        w1 = H1[:, :, :, :].rearrange("p a f t -> p (a f t)").rearrange("p (e f) -> p e f", e=E)
        stC = sb("stC", [P, NT, 6])
        mvC = sb("mvC", [P, NT, 2])
        rsC = sb("rsC", [P, 4, NT])
        EX = sb("EX", [P, NT, E])
        PR = sb("PR", [P, NT, E])
        M8 = sb("M8", [P, NT, 8])
        I8 = sb("I8", [P, NT, 8], U32)
        IF = sb("IF", [P, NT, 2])
        K0 = sb("K0", [P, NT, E])
        K1 = sb("K1", [P, NT, E])
        g1 = sb("g1", [P, NT])
        g2 = sb("g2", [P, NT])
        WT = sb("WT", [P, NT, E])
        WTT = CXT[0:E, :]

        psA = bank("psA", [P, T])
        psS = bank("psS", [P, 2, T])
        psT = bank("psT", [P, 2, T])
        psV = bank("psV", [P, T])
        psH = bank("psH", [P, T])
        psY = bank("psY", [P, T])

        s_vec = sem("s_vec")
        s_sq = sem("s_sq")
        s_w1 = sem("s_w1")
        s_w2 = sem("s_w2")
        s_ident = sem("s_ident")
        s_const = sem("s_const")
        s_colT = sem("s_colT")
        s_cols = sem("s_cols")
        s_dec = sem("s_dec")
        s_wrow = sem("s_wrow")
        s_w1s = sem("s_w1s")

        (U_ZA, U_K, U_V, U_R, U_WO, U_XC, U_KK), U_RR = range(7), 6 + NF
        U_KV, U_ZH, U_Q, U_KP, U_VP, U_KT = range(U_RR + 1, U_RR + 7)
        U_QT = U_KT + NG
        NA = U_QT + NG
        a_full = sig("a_full", NA)
        a_taken = sig("a_taken", NA)
        x_in = sig("x_in", 16)
        x_used = sig("x_used")
        a_stats = sig("a_stats", 3)
        a_rstd = sig("a_rstd", 3)
        za_ready = sig("za_ready", 3)
        d_ready = sig("d_ready", 2)
        mix_ready = sig("mix_ready", 5)
        args_ready = sig("args_ready")
        exps_ready = sig("exps_ready")
        side_ready = sig("side_ready", 2)
        g_ready = sig("g_ready")
        kk_ready = sig("kk_ready", NF)
        z1_ready = sig("z1_ready")
        hi_ready = sig("hi_ready", 2)
        hi_copied = sig("hi_copied", 2)

        NS, NX = NG * NT * G, NG * (NT * G + 1)
        s_full = sig("s_full", NS)
        s_taken = sig("s_taken", NS)
        t_full = sig("t_full", NX)
        t_taken = sig("t_taken", NX)
        m_ready = sig("m_ready", NG)
        v_full = sig("v_full", NG * NT)
        c_full = sig("c_full", NG)
        ct_ready = sig("ct_ready", NG)
        cx_ready = sig("cx_ready", NG)
        kept = sig("kept")

        NH, NY = 3 + E * NF, 3 + E
        h_full = sig("h_full", NH)
        h_taken = sig("h_taken", NH)
        y_full = sig("y_full", NY)
        y_taken = sig("y_taken", NY)
        c_stats = sig("c_stats")
        c_rstd = sig("c_rstd")
        zm_ready = sig("zm_ready")
        ml_ready = sig("ml_ready")
        ex_ready = sig("ex_ready")
        wt_ready = sig("wt_ready")
        out_done = sig("out_done", 16)

        dve_a, dve_b, dve_c = sem("dve_a"), sem("dve_b"), sem("dve_c")
        pool_a, pool_c = sem("pool_a"), sem("pool_c")

        def chunk(ap, c):
            return ap[:, c * P:(c + 1) * P]

        def heads(ap):
            return ap.rearrange("p (c h d) -> p c h d", h=H, d=DH)

        def tokens(ap):
            return ap.rearrange("p (c n) -> p c n", c=NT)

        def apart(engine):
            idle_turn[0] = (idle_turn[0] + 1) % 16
            unread = idle[:, idle_turn[0]:idle_turn[0] + 1]
            if engine is nc.gpsimd:
                engine.tensor_tensor(unread, half[:, 0:1], half[:, 0:1], ALU.mult)
            else:
                engine.tensor_copy(unread, half[:, 0:1])

        def over(engine, body):
            body(0)
            with engine.Fori(1, B) as b:
                body(b)

        block = ctx.enter_context(nc.Block())

        @block.sync
        def _(sp):
            for i, n in enumerate(VEC):
                sp.dma_start(rows[i:i + 1, :], t[n].rearrange("(a n) -> a n", a=1)).then_inc(s_vec, 16)
            sp.dma_start(rows[NV:NV + E * NF, :],
                         t["L0_ffn_b1"].rearrange("e (c p) -> (e c) p", p=P)).then_inc(s_vec, 16)

            def load(b):
                after(sp, x_used, b, 0)
                sp.dma_start(X[:, :, :], x[b].rearrange("(c p) n -> p c n", p=P)).then_inc(x_in.sem, 16)

            def store(b):
                after(sp, y_taken, b, NY)
                sp.dma_start(out[b].rearrange("(c p) n -> p c n", p=P), RES[:, :, :]).then_inc(out_done.sem, 16)

            load(0)
            for n in SQUARE:
                sp.dma_start(sq[n][:, :], t[n]).then_inc(s_sq, 16)
            sp.dma_start(wck[:, :], t["L0_attn_Wck"]).then_inc(s_sq, 16)
            sp.dma_start(wcv[:, :, :], t["L0_attn_Wcv"].rearrange("(c p) n -> p c n", p=P)).then_inc(s_sq, 16)
            sp.dma_start(wg[:, :], t["L0_ffn_Wg"]).then_inc(s_sq, 16)
            sp.dma_start(b2[:, :], t["L0_ffn_b2"]).then_inc(s_sq, 16)
            sp.dma_start(w1, t["L0_ffn_W1"].rearrange("e p f -> p e f")).then_inc(s_w1, 16)
            sp.dma_start(w2[:, :, :, :], t["L0_ffn_W2"].rearrange("e (c p) n -> p e c n", p=P)).then_inc(s_w2, 16)
            with sp.Fori(1, B) as b:
                load(b)
                store(b - 1)
            store(B - 1)
            sp.wait_ge(out_done.sem, out_done.at(B - 1, 16))

        N_VEC, N_SQ, N_CONST = 16 * (NV + 1), 16 * (len(SQUARE) + 4), 10 + E

        @block.gpsimd
        def _(pool):
            pool.memset(ident[:, :], 0.0).then_inc(s_ident, 1)
            pool.wait_ge(s_ident, 1)
            pool.affine_select(out=ident[:, :], in_=ident[:, :], compare_op=ALU.not_equal, fill=1.0, base=0,
                               pattern=[[-1, P]], channel_multiplier=1).then_inc(s_ident, 1)
            pool.memset(half[:, :], -0.5).then_inc(s_const, 1)
            for e in range(E):
                pool.memset(iota[:, e:e + 1], float(e)).then_inc(s_const, 1)
            pool.memset(XA[:, 0:1], 0.0).then_inc(s_const, 1)
            pool.memset(PP[:, 0:1], NEG).then_inc(s_const, 1)
            pool.memset(AA[:, 0:1], 0.0).then_inc(s_const, 1)
            pool.memset(BB[:, 0:1], 0.0).then_inc(s_const, 1)
            pool.memset(QA[:, :, :, RS:HW], 0.0).then_inc(s_const, 1)
            pool.memset(KA[:, :, :, RM:HW], 0.0).then_inc(s_const, 1)
            pool.memset(KA[:, :, :, RS:RM], 1.0).then_inc(s_const, 1)
            pool.memset(VA[:, :, :, DH + 1:HW], 0.0).then_inc(s_const, 1)
            pool.memset(VA[:, :, :, DH:DH + 1], 1.0).then_inc(s_const, 1)
            pool.wait_ge(s_const, N_CONST)

            own_a = Chain(pool, pool_a, 13)
            own_c = Chain(pool, pool_c, 1)

            def rstd(own, mv, rs, both):
                var = mv[:, :, 1]
                own.link(pool.tensor_scalar(rs[:, 1, :], var, EPS, None, ALU.add))
                last = pool.tensor_tensor(rs[:, 0, :], rs[:, 1, :], half[:, :], ALU.pow)
                if not both:
                    return last
                own.link(last)
                own.link(pool.tensor_tensor(rs[:, 1, :], rs[:, 0, :], rs[:, 0, :], ALU.mult))
                own.step(pool.tensor_tensor(rs[:, 1, :], rs[:, 1, :], var, ALU.mult))
                own.wait()
                apart(pool)
                own.link(pool.tensor_scalar(rs[:, 1, :], rs[:, 1, :], EPS, None, ALU.add))
                own.link(pool.tensor_tensor(rs[:, 2, :], rs[:, 1, :], half[:, :], ALU.pow))
                return pool.tensor_tensor(rs[:, 3, :], rs[:, 2, :], rs[:, 0, :], ALU.mult)

            def shift(b, u):
                after(pool, a_taken, b, u + 1)
                pool.tensor_tensor(D[:, :], XA[:, 1:T + 1], XA[:, 0:T], ALU.subtract).then_inc(d_ready.sem, 1)

            def a0(b):
                own_a.begin(b)
                after(pool, a_stats, b, 1)
                apart(pool)
                rstd(own_a, mvA, rsA, True).then_inc(a_rstd.sem, 1)

            def a1(b):
                shift(b, U_ZA)

            def a2(b):
                after(pool, a_taken, b, U_R + 1)
                apart(pool)
                pool.tensor_scalar(R[:, :], R[:, :], 0.5, 0.5, ALU.mult, ALU.add).then_inc(side_ready.sem, 1)

            def a3(b):
                after(pool, exps_ready, b, 1)
                pool.tensor_tensor(N2[:, :], EE[:, 3, :], V[:, :], ALU.mult).then_inc(side_ready.sem, 1)

            def a4(b):
                after(pool, a_stats, b, 2)
                apart(pool)
                rstd(own_a, mvA, rsA, False).then_inc(a_rstd.sem, 1)

            def a5(b):
                shift(b, U_XC)
                for f in range(NF):
                    after(pool, a_taken, b, U_KK + f + 1)
                    pool.tensor_tensor(KK[:, f, :], KK[:, f, :], KK[:, f, :], ALU.mult).then_inc(kk_ready.sem, 1)

            def a6(b):
                after(pool, a_stats, b, 3)
                apart(pool)
                rstd(own_a, mvA, rsA, True).then_inc(a_rstd.sem, 1)

            def a7(b):
                after(pool, hi_ready, b, 1)
                apart(pool)
                pool.tensor_copy(QA[:, :, :, DH:2 * DH], QA[:, :, :, 0:DH]).then_inc(hi_copied.sem, 1)
                after(pool, hi_ready, b, 2)
                apart(pool)
                pool.tensor_copy(KA[:, :, :, 2 * DH:RS], KA[:, :, :, 0:DH]).then_inc(hi_copied.sem, 1)
                own_a.end()

            def keep(b):
                after(pool, z1_ready, b, 1)
                after(pool, y_taken, b - 1, 1)
                pool.tensor_tensor(XZ[:, :, :], X1[:, :, :], Z1[:, :, :], ALU.add)
                pool.tensor_scalar(Z1b[:, :, :], Z1[:, :, :], 1.0, None, ALU.mult).then_inc(kept.sem, 1)

            def c_norm(b):
                own_c.begin(b)
                after(pool, c_stats, b, 1)
                apart(pool)
                rstd(own_c, mvC, rsC, False).then_inc(c_rstd.sem, 1)
                own_c.end()

            def c_split(b):
                after(pool, h_taken, b, 2)
                pool.tensor_tensor(ML[:, :], MT[:, :], MH[:, :].bitcast(F32), ALU.subtract).then_inc(ml_ready.sem, 1)

            def element(b):
                for step in (a0, a1, a2, a3, a4, a5, a6, a7, keep, c_norm, c_split):
                    step(b)

            over(pool, element)

        @block.scalar
        def _(act):
            act.wait_ge(s_colT, 1)
            act.activation(cols[:, :], psA[:, 0:NV + E * NF], ACT.Copy).then_inc(s_cols, 1)
            act.wait_ge(s_cols, 1)
            act.activation(wdec[:, :], col["L0_attn_time_decay"], ACT.Exp).then_inc(s_dec, 1)
            act.wait_ge(s_const, N_CONST)

            def affine(dst, src, g, c):
                return act.activation(dst, src, ACT.Identity, bias=col[c], scale=col[g])

            def take(b, u, f):
                after(act, a_full, b, u + 1)
                f().then_inc(a_taken.sem, 1)

            def a0(b):
                take(b, U_ZA, lambda: affine(XA[:, 1:T + 1], psA[:, :], "L0_attn_ln0_g", "L0_attn_ln0_b"))

            def a1(b):
                take(b, U_K, lambda: act.activation(K[:, :], psA[:, :], ACT.Copy))
                take(b, U_V, lambda: act.activation(V[:, :], psA[:, :], ACT.Copy))
                take(b, U_R, lambda: act.activation(R[:, :], psA[:, :], ACT.Tanh, scale=0.5))

            def a2(b):
                after(act, args_ready, b, 1)
                act.activation(EE[:, :, :], EE[:, :, :], ACT.Exp).then_inc(exps_ready.sem, 1)

            def a4(b):
                take(b, U_XC, lambda: affine(XA[:, 1:T + 1], psA[:, :], "L0_attn_ln1_g", "L0_attn_ln1_b"))

            def a5(b):
                for f in range(NF):
                    take(b, U_KK + f, lambda: act.activation(KK[:, f, :], psA[:, :], ACT.Relu))
                take(b, U_RR, lambda: act.activation(RT[:, :, :], tokens(psA[:, :]), ACT.Tanh, scale=0.5))

            def a7(b):
                take(b, U_ZH, lambda: affine(HT[:, :], psA[:, :], "L0_ffn_ln1_g", "L0_ffn_ln1_b"))
                after(act, v_full, b, 0)
                take(b, U_VP, lambda: act.activation(VA[:, :, :, 0:DH], heads(psA[:, :]), ACT.Copy))
                for g in range(NG):
                    take(b, U_KT + g, lambda: act.activation(KT[:, g, :], psA[:, :], ACT.Copy))

            def q2(b, g):
                n = g * (NT * G + 1)
                after(act, t_full, b, n + 1)
                act.activation(Q2[:, g % 2, :], psT[:, n % 2, :], ACT.Copy).then_inc(t_taken.sem, 1)

            def exps(b, g, c):
                for j in range(G):
                    n = g * (NT * G + 1) + 1 + c * G + j
                    if j == 0:
                        after(act, v_full, b, g * NT + c - 1)
                    after(act, t_full, b, n + 1)
                    act.activation(PT[:, (c % 2) * G + j, :], psT[:, n % 2, :], ACT.Exp,
                                   scale=SCALE).then_inc(t_taken.sem, 1)

            def c_ctx(b):
                after(act, h_full, b, 1)
                act.activation(CXT[:, :], psH[:, :], ACT.Copy).then_inc(h_taken.sem, 1)

            def c_norm(b):
                after(act, h_full, b, 2)
                affine(MH[:, :], psH[:, :], "L0_ffn_ln2_g", "L0_ffn_ln2_b")
                affine(MT[:, :], psH[:, :], "L0_ffn_ln2_g", "L0_ffn_ln2_b").then_inc(h_taken.sem, 1)

            def c_gate(b):
                after(act, y_taken, b, 2)
                act.activation(EX[:, :, :], EX[:, :, :], ACT.Exp).then_inc(ex_ready.sem, 1)

            def c_gate_t(b):
                after(act, h_full, b, 3)
                act.activation(WTT, psH[0:E, :], ACT.Copy).then_inc(h_taken.sem, 1)

            def gelus(b, e):
                if True:
                    after(act, y_full, b, 3 + e - 1)
                for f in range(NF):
                    n = 3 + e * NF + f
                    after(act, h_full, b, n + 1)
                    act.activation(H1[:, e % 2, f, :], psH[:, :], ACT.Gelu_apprx_tanh,
                                   bias=cols[:, NV + e * NF + f:NV + e * NF + f + 1]).then_inc(h_taken.sem, 1)

            def element(b):
                for step in (a0, a1, a2, a4, a5, a7):
                    step(b)
                for g in range(NG):
                    q2(b, g)
                    for c in range(NT):
                        exps(b, g, c)
                for step in (c_ctx, c_norm, c_gate, c_gate_t):
                    step(b)
                for e in range(E):
                    gelus(b, e)

            over(act, element)

        @block.tensor
        def _(pe):
            pe.wait_ge(s_ident, 2)
            pe.wait_ge(s_vec, N_VEC)
            pe.transpose(psA[:, 0:NV + E * NF], rows[:, :], ident[0:NV + E * NF, 0:NV + E * NF]).then_inc(s_colT, 1)
            pe.wait_ge(s_cols, 1)
            pe.wait_ge(s_const, N_CONST)
            pe.wait_ge(s_sq, N_SQ)

            def in_a(b, u, f):
                after(pe, a_taken, b, u)
                f().then_inc(a_full.sem, 1)

            def transposes(dst, src):
                for c in range(NT):
                    last = pe.transpose(chunk(dst, c), src[:, c, :], ident[:, :])
                return last

            def to_tokens(dst, src, w):
                for c in range(NT):
                    last = pe.matmul(chunk(dst, c), chunk(src, c), w, start=True, stop=True)
                return last

            def a0(b):
                after(pe, za_ready, b, 1)
                in_a(b, U_ZA, lambda: transposes(psA, ZA))

            def a1(b):
                for i, (n, m) in enumerate((("L0_attn_Wk", MK), ("L0_attn_Wv", MV), ("L0_attn_Wr", MR))):
                    after(pe, mix_ready, b, i + 1)
                    in_a(b, U_K + i, lambda: pe.matmul(psA[:, :], sq[n][:, :], m[:, :], start=True, stop=True))

            def a4(b):
                after(pe, g_ready, b, 1)
                in_a(b, U_WO, lambda: to_tokens(psA, GT, sq["L0_attn_Wo"][:, :]))
                after(pe, za_ready, b, 2)
                in_a(b, U_XC, lambda: transposes(psA, ZA))

            def a5(b):
                after(pe, mix_ready, b, 4)
                for f in range(NF):
                    in_a(b, U_KK + f, lambda: pe.matmul(psA[:, :], chunk(wck, f), MK[:, :], start=True, stop=True))
                after(pe, mix_ready, b, 5)
                in_a(b, U_RR, lambda: to_tokens(psA, MR, sq["L0_attn_Wcr"][:, :]))

            def channel_mix_out():
                for c in range(NT):
                    for f in range(NF):
                        last = pe.matmul(chunk(psA, c), chunk(KK[:, f, :], c), wcv[:, f, :],
                                         start=(f == 0), stop=(f == NF - 1))
                return last

            def a6(b):
                after(pe, kk_ready, b, NF)
                in_a(b, U_KV, channel_mix_out)

            def a7(b):
                after(pe, za_ready, b, 3)
                in_a(b, U_ZH, lambda: transposes(psA, ZA))
                after(pe, a_taken, b, U_ZH + 1)
                for u, n in ((U_Q, "L0_ffn_Wq"), (U_KP, "L0_ffn_Wk"), (U_VP, "L0_ffn_Wv")):
                    in_a(b, u, lambda: to_tokens(psA, HT, sq[n][:, :]))
                after(pe, hi_copied, b, 2)
                for u, s in ((U_KT, KA), (U_QT, QA)):
                    for g in range(NG):
                        in_a(b, u + g, lambda: transposes(
                            psA, s[:, :, g * G:(g + 1) * G, :].rearrange("p c h w -> p c (h w)")))

            def scores(b, g, c):
                for j in range(G):
                    n = (g * NT + c) * G + j
                    after(pe, s_taken, b, n - 1)
                    r = slice(j * HW, j * HW + RS)
                    pe.matmul(psS[:, n % 2, :], chunk(Q1[r, g, :], c), KT[r, g, :],
                              start=True, stop=True).then_inc(s_full.sem, 1)

            def q2(b, g):
                n = g * (NT * G + 1)
                after(pe, m_ready, b, g + 1)
                after(pe, t_taken, b, n - 1)
                transposes(psT[:, n % 2, :], QA[:, :, g * G:(g + 1) * G, :].rearrange(
                    "p c h w -> p c (h w)")).then_inc(t_full.sem, 1)

            def scores_t(b, g, c):
                if c == 0:
                    after(pe, t_taken, b, g * (NT * G + 1) + 1)
                for j in range(G):
                    n = g * (NT * G + 1) + 1 + c * G + j
                    after(pe, t_taken, b, n - 1)
                    r = slice(j * HW, j * HW + RM)
                    pe.matmul(psT[:, n % 2, :], chunk(KT[r, g, :], c), Q2[r, g % 2, :],
                              start=True, stop=True).then_inc(t_full.sem, 1)

            def times_v(b, g, c):
                after(pe, t_taken, b, g * (NT * G + 1) + 1 + (c + 1) * G)
                if c == 0:
                    after(pe, cx_ready, b, g)
                for j in range(G):
                    r = slice(j * HW, (j + 1) * HW)
                    last = pe.matmul(psV[r, :], VA[:, c, g * G + j, :], PT[:, (c % 2) * G + j, :],
                                     start=(c == 0), stop=(c == NT - 1))
                last.then_inc(v_full.sem, 1)

            def context(b, g):
                after(pe, ct_ready, b, g + 1)
                for c in range(NT):
                    last = pe.transpose(chunk(psV, c), chunk(CT, c), ident[:, :])
                last.then_inc(c_full.sem, 1)

            def c_ctx(b):
                after(pe, cx_ready, b, NG)
                after(pe, h_taken, b, 0)
                transposes(psH, CX[:, :, :, :].rearrange("p c h d -> p c (h d)")).then_inc(h_full.sem, 1)
                after(pe, h_taken, b, 1)
                after(pe, y_taken, b, 0)
                to_tokens(psY, CXT, sq["L0_ffn_Wo"][:, :]).then_inc(y_full.sem, 1)

            def c_norm(b):
                after(pe, zm_ready, b, 1)
                transposes(psH, ZM).then_inc(h_full.sem, 1)
                after(pe, h_taken, b, 2)
                after(pe, y_taken, b, 1)
                for c in range(NT):
                    last = pe.matmul(psY[:, c * E:(c + 1) * E], chunk(MT, c), wg[:, :], start=True, stop=True)
                last.then_inc(y_full.sem, 1)

            def c_gate(b):
                after(pe, wt_ready, b, 1)
                for c in range(NT):
                    last = pe.transpose(chunk(psH[0:E, :], c), WT[:, c, :], ident[:, :])
                last.then_inc(h_full.sem, 1)
                after(pe, h_taken, b, 3)
                after(pe, y_taken, b, 2)
                to_tokens(psY, WTT, b2[:, :]).then_inc(y_full.sem, 1)

            def hidden(b, e, f):
                if e == 0 and f == 0:
                    after(pe, ml_ready, b, 1)
                    pe.wait_ge(s_w1s, 1)
                after(pe, h_taken, b, 3 + e * NF + f)
                w = slice(f * P, (f + 1) * P)
                pe.matmul(psH[:, :], w1h[:, e, w], MH[:, :], start=True, stop=False)
                pe.matmul(psH[:, :], w1h[:, e, w], ML[:, :], start=False, stop=False)
                pe.matmul(psH[:, :], w1l[:, e, w], MH[:, :], start=False, stop=True).then_inc(h_full.sem, 1)

            def expert(b, e):
                if e == 0:
                    pe.wait_ge(s_w2, 16)
                after(pe, h_taken, b, 3 + (e + 1) * NF)
                after(pe, y_taken, b, 3 + e)
                for c in range(NT):
                    for f in range(NF):
                        last = pe.matmul(chunk(psY, c), chunk(H1[:, e % 2, f, :], c), w2[:, e, f, :],
                                         start=(f == 0), stop=(f == NF - 1))
                last.then_inc(y_full.sem, 1)

            def element(b):
                for step in (a0, a1, a4, a5, a6, a7):
                    step(b)
                for c in range(NT):
                    scores(b, 0, c)
                for g in range(NG):
                    if g + 1 < NG:
                        for c in range(NT):
                            scores(b, g + 1, c)
                    q2(b, g)
                    for c in range(NT):
                        scores_t(b, g, c)
                        if c:
                            times_v(b, g, c - 1)
                    times_v(b, g, NT - 1)
                    context(b, g)
                for step in (c_ctx, c_norm, c_gate):
                    step(b)
                for e in range(E):
                    for f in range(NF):
                        hidden(b, e, f)
                    if e:
                        expert(b, e - 1)
                expert(b, E - 1)

            over(pe, element)

        @block.vector
        def _(dve):
            own_a = Chain(dve, dve_a, 14)
            own_b = Chain(dve, dve_b, 2 * NG)
            own_c = Chain(dve, dve_c, 14)
            dve.wait_ge(s_dec, 1)
            dve.tensor_scalar(wdec[:, :], wdec[:, :], -1.0, None, ALU.mult).then_inc(s_wrow, 1)
            dve.memset(wrow[:, :], 0.0).then_inc(s_wrow, 1)
            dve.wait_ge(s_wrow, 2)
            dve.tensor_scalar(wrow[:, :], wrow[:, :], wdec[:, 0:1], None, ALU.add).then_inc(s_wrow, 1)
            dve.wait_ge(s_wrow, 3)
            dve.wait_ge(s_const, N_CONST)

            def split_w1():
                dve.wait_ge(s_w1, 16)
                dve.tensor_copy(w1h[:, :, :], w1).then_inc(s_wrow, 1)
                dve.wait_ge(s_wrow, 4)
                dve.tensor_tensor(w1l[:, :, :], w1, w1h[:, :, :].bitcast(F32), ALU.subtract).then_inc(s_w1s, 1)

            def stats(own, src, st, mv):
                for c in range(NT):
                    last = dve.bn_stats(st[:, c, :], src[:, c, :])
                own.step(last)
                own.wait()
                apart(dve)
                for c in range(NT):
                    last = dve.bn_aggr(mv[:, c, :], st[:, c, :])
                return last

            def normed(dst, src, mv, rs):
                for c in range(NT):
                    last = dve.tensor_scalar(dst[:, c, :], src[:, c, :], mv[:, c, 0:1], rs[:, c:c + 1],
                                             ALU.subtract, ALU.mult)
                return last

            def mix(dst, name):
                return dve.scalar_tensor_tensor(out=dst[:, :], in0=D[:, :], scalar=col[name], in1=XA[:, 0:T],
                                                op0=ALU.mult, op1=ALU.add)

            def a0(b):
                own_a.begin(b)
                dve.wait_ge(x_in.sem, x_in.at(b, 16))
                stats(own_a, X, stA, mvA).then_inc(a_stats.sem, 1)
                after(dve, a_rstd, b, 1)
                normed(ZA, X, mvA, rsA[:, 3, :]).then_inc(za_ready.sem, 1)
                normed(Z0, X, mvA, rsA[:, 0, :])

            def a1(b):
                after(dve, d_ready, b, 1)
                for m, n in ((MK, "L0_attn_tm_k"), (MV, "L0_attn_tm_v"), (MR, "L0_attn_tm_r")):
                    mix(m, n).then_inc(mix_ready.sem, 1)

            def a2(b):
                after(dve, a_taken, b, U_K + 1)
                own_a.link(dve.tensor_tensor_scan(PP[:, 1:T + 1], wrow[:, :], K[:, :], NEG, ALU.add, ALU.max))
                dve.scalar_tensor_tensor(out=EE[:, 0, :], in0=PP[:, 0:T], scalar=wdec[:, 0:1], in1=PP[:, 1:T + 1],
                                         op0=ALU.add, op1=ALU.subtract)
                dve.tensor_tensor(EE[:, 1, :], K[:, :], PP[:, 1:T + 1], ALU.subtract)
                own_a.link(dve.scalar_tensor_tensor(out=DD[:, :], in0=K[:, :], scalar=col["L0_attn_time_first"],
                                                    in1=PP[:, 0:T], op0=ALU.add, op1=ALU.subtract))
                dve.tensor_scalar(EE[:, 2, :], DD[:, :], 0.0, -1.0, ALU.max, ALU.mult)
                dve.tensor_scalar(EE[:, 3, :], DD[:, :], 0.0, None, ALU.min).then_inc(args_ready.sem, 1)

            def a3(b):
                after(dve, exps_ready, b, 1)
                after(dve, a_taken, b, U_V + 1)
                own_a.link(dve.tensor_tensor(EV[:, :], EE[:, 1, :], V[:, :], ALU.mult))
                dve.tensor_tensor_scan(BB[:, 1:T + 1], EE[:, 0, :], EE[:, 1, :], 0.0, ALU.mult, ALU.add)
                own_a.link(dve.tensor_tensor_scan(AA[:, 1:T + 1], EE[:, 0, :], EV[:, :], 0.0, ALU.mult, ALU.add))
                dve.tensor_tensor(N1[:, :], EE[:, 2, :], AA[:, 0:T], ALU.mult)
                own_a.link(dve.tensor_tensor(D1[:, :], EE[:, 2, :], BB[:, 0:T], ALU.mult))
                own_a.link(dve.tensor_tensor(D1[:, :], D1[:, :], EE[:, 3, :], ALU.add))
                own_a.link(dve.reciprocal(D1[:, :], D1[:, :]))
                after(dve, side_ready, b, 2)
                own_a.link(dve.tensor_tensor(N1[:, :], N1[:, :], N2[:, :], ALU.add))
                own_a.link(dve.tensor_tensor(N1[:, :], N1[:, :], D1[:, :], ALU.mult))
                dve.tensor_tensor(GT[:, :], N1[:, :], R[:, :], ALU.mult).then_inc(g_ready.sem, 1)

            def a4(b):
                after(dve, a_full, b, U_WO + 1)
                dve.tensor_tensor(Y1[:, :, :], tokens(psA[:, :]), Z0[:, :, :], ALU.add).then_inc(a_taken.sem, 1)
                after(dve, a_taken, b, U_WO + 1)
                stats(own_a, Y1, stA, mvA).then_inc(a_stats.sem, 1)
                after(dve, a_rstd, b, 2)
                normed(ZA, Y1, mvA, rsA[:, 0, :]).then_inc(za_ready.sem, 1)

            def a5(b):
                after(dve, d_ready, b, 2)
                for m, n in ((MK, "L0_attn_cm_k"), (MR, "L0_attn_cm_r")):
                    mix(m, n).then_inc(mix_ready.sem, 1)

            def a6(b):
                after(dve, a_taken, b, U_RR + 1)
                own_a.link(dve.tensor_scalar(RT[:, :, :], RT[:, :, :], 0.5, 0.5, ALU.mult, ALU.add))
                after(dve, a_full, b, U_KV + 1)
                dve.tensor_tensor(RT[:, :, :], tokens(psA[:, :]), RT[:, :, :], ALU.mult).then_inc(a_taken.sem, 1)
                own_a.link(dve.tensor_tensor(Y1[:, :, :], Y1[:, :, :], X[:, :, :], ALU.add))
                after(dve, a_taken, b, U_KV + 1)
                after(dve, kept, b, 0)
                dve.tensor_tensor(X1[:, :, :], RT[:, :, :], Y1[:, :, :], ALU.add).then_inc(x_used.sem, 1)
                after(dve, x_used, b, 1)
                stats(own_a, X1, stA, mvA).then_inc(a_stats.sem, 1)
                after(dve, a_rstd, b, 3)
                normed(ZA, X1, mvA, rsA[:, 3, :]).then_inc(za_ready.sem, 1)
                normed(Z1, X1, mvA, rsA[:, 0, :]).then_inc(z1_ready.sem, 1)

            def a7(b):
                after(dve, t_full, b - 1, (NG - 1) * (NT * G + 1) + 1)
                for u, s, lo in ((U_Q, QA, 2 * DH), (U_KP, KA, DH)):
                    after(dve, a_full, b, u + 1)
                    dve.tensor_copy(s[:, :, :, 0:DH].bitcast(F32R), heads(psA[:, :])).then_inc(hi_ready.sem, 1)
                    after(dve, hi_ready, b, 1 if s is QA else 2)
                    dve.tensor_tensor(s[:, :, :, lo:lo + DH], heads(psA[:, :]), s[:, :, :, 0:DH],
                                      ALU.subtract).then_inc(a_taken.sem, 1)
                for g in range(NG):
                    after(dve, a_full, b, U_QT + g + 1)
                    dve.tensor_copy(Q1[:, g, :], psA[:, :]).then_inc(a_taken.sem, 1)
                own_a.end()

            def maxima(b, g, c):
                if g == 0 and c == 0:
                    own_b.begin(b)
                for j in range(G):
                    n = (g * NT + c) * G + j
                    after(dve, s_full, b, n + 1)
                    dve.tensor_reduce(NM[:, c, g * G + j:g * G + j + 1], psS[:, n % 2, :], AX_X, ALU.max,
                                      negate=True).then_inc(s_taken.sem, 1)
                if c == NT - 1:
                    after(dve, s_taken, b, (g + 1) * NT * G)
                    hs = slice(g * G, (g + 1) * G)
                    own_b.link(dve.tensor_copy(QA[:, :, hs, RS].bitcast(F32R), NM[:, :, hs]))
                    dve.tensor_tensor(QA[:, :, hs, RS + 1], NM[:, :, hs], QA[:, :, hs, RS],
                                      ALU.subtract).then_inc(m_ready.sem, 1)

            def context(b, g):
                after(dve, v_full, b, (g + 1) * NT)
                dve.tensor_copy(CT[:, :], psV[:, :]).then_inc(ct_ready.sem, 1)
                after(dve, c_full, b, g + 1)
                if g == 0:
                    after(dve, h_full, b - 1, 1)
                ctx4 = psV[:, :].rearrange("p (c j w) -> p c j w", c=NT, w=HW)
                own_b.link(dve.reciprocal(RD[:, :, :], ctx4[:, :, :, DH]))
                dve.tensor_tensor(CX[:, :, g * G:(g + 1) * G, :], ctx4[:, :, :, 0:DH],
                                  RD[:, :, :].unsqueeze(3).to_broadcast([P, NT, G, DH]), ALU.mult).then_inc(cx_ready.sem, 1)
                if g == NG - 1:
                    own_b.end()

            def c_ctx(b):
                own_c.begin(b)
                after(dve, kept, b, 1)
                after(dve, out_done, b, 0)
                after(dve, y_full, b, 1)
                own_c.link(dve.tensor_tensor(Y3[:, :, :], tokens(psY[:, :]), Z1b[:, :, :], ALU.add))
                dve.tensor_tensor(RES[:, :, :], tokens(psY[:, :]), XZ[:, :, :], ALU.add).then_inc(y_taken.sem, 1)
                stats(own_c, Y3, stC, mvC).then_inc(c_stats.sem, 1)
                after(dve, c_rstd, b, 1)
                normed(ZM, Y3, mvC, rsC[:, 0, :]).then_inc(zm_ready.sem, 1)

            def bc(v):
                return v.unsqueeze(2).to_broadcast([P, NT, E])

            def c_gate(b):
                after(dve, y_full, b, 2)
                logits = psY[:, 0:NT * E].rearrange("p (c e) -> p c e", e=E)
                own_c.link(dve.tensor_reduce(g1[:, :], logits, AX_X, ALU.max))
                dve.tensor_tensor(EX[:, :, :], logits, bc(g1[:, :]), ALU.subtract).then_inc(y_taken.sem, 1)
                after(dve, ex_ready, b, 1)
                own_c.link(dve.tensor_reduce(g1[:, :], EX[:, :, :], AX_X, ALU.add))
                own_c.link(dve.reciprocal(g2[:, :], g1[:, :]))
                own_c.step(dve.tensor_tensor(PR[:, :, :], EX[:, :, :], bc(g2[:, :]), ALU.mult))
                own_c.wait()
                apart(dve)
                for c in range(NT):
                    last = dve.max(M8[:, c, :], PR[:, c, :])
                own_c.step(last)
                own_c.wait()
                apart(dve)
                for c in range(NT):
                    last = dve.max_index(I8[:, c, :], M8[:, c, :], PR[:, c, :])
                own_c.link(last)
                own_c.link(dve.tensor_copy(IF[:, :, :], I8[:, :, 0:2]))
                experts = iota[:, :].unsqueeze(1).to_broadcast([P, NT, E])
                dve.tensor_tensor(K0[:, :, :], experts, bc(IF[:, :, 0]), ALU.is_equal)
                own_c.link(dve.tensor_tensor(K1[:, :, :], experts, bc(IF[:, :, 1]), ALU.is_equal))
                own_c.link(dve.tensor_tensor(K0[:, :, :], K0[:, :, :], K1[:, :, :], ALU.add))
                own_c.link(dve.tensor_tensor(K1[:, :, :], PR[:, :, :], K0[:, :, :], ALU.mult))
                own_c.link(dve.tensor_reduce(g1[:, :], K1[:, :, :], AX_X, ALU.add))
                own_c.link(dve.reciprocal(g2[:, :], g1[:, :]))
                dve.tensor_tensor(WT[:, :, :], K1[:, :, :], bc(g2[:, :]), ALU.mult).then_inc(wt_ready.sem, 1)

            def c_bias(b):
                after(dve, y_full, b, 3)
                after(dve, y_taken, b, 1)
                dve.tensor_tensor(RES[:, :, :], tokens(psY[:, :]), RES[:, :, :], ALU.add).then_inc(y_taken.sem, 1)

            def add_expert(b, e):
                after(dve, y_full, b, 4 + e)
                after(dve, y_taken, b, 3 + e)
                if e == 0:
                    after(dve, wt_ready, b, 1)
                for c in range(NT):
                    last = dve.scalar_tensor_tensor(out=RES[:, c, :], in0=chunk(psY, c), scalar=WT[:, c, e:e + 1],
                                                    in1=RES[:, c, :], op0=ALU.mult, op1=ALU.add)
                last.then_inc(y_taken.sem, 1)
                if e == E - 1:
                    own_c.end()

            def element(b):
                for step in (a0, a1, a2, a3, a4, a5, a6, a7):
                    step(b)
                if isinstance(b, int):
                    split_w1()
                for c in range(NT):
                    maxima(b, 0, c)
                for g in range(NG):
                    if g + 1 < NG:
                        for c in range(NT):
                            maxima(b, g + 1, c)
                    context(b, g)
                for step in (c_ctx, c_gate, c_bias):
                    step(b)
                for e in range(E):
                    add_expert(b, e)

            over(dve, element)


_INS = VEC + SQUARE + ["L0_attn_x", "L0_attn_Wck", "L0_attn_Wcv", "L0_ffn_Wg", "L0_ffn_W1", "L0_ffn_b1",
                       "L0_ffn_W2", "L0_ffn_b2"]


def kernel(**inputs):
    import numpy as _np
    import concourse.bacc as _bacc
    from concourse import mybir as _mybir
    from concourse.bass_utils import run_bass_kernel_spmd as _run

    nc = _bacc.Bacc("TRN2", target_bir_lowering=False, num_devices=1)
    arrays, args = {}, {}
    for name in _INS:
        a = _np.ascontiguousarray(inputs[name])
        arrays[f"in_{name}_dram"] = a
        args[name] = nc.dram_tensor(f"in_{name}_dram", a.shape, _mybir.dt.from_np(a.dtype), kind="ExternalInput").ap()
    shape = inputs["L0_attn_x"].shape
    out = nc.dram_tensor("out_0_dram", shape, _mybir.dt.float32, kind="ExternalOutput").ap()
    build(nc, args, out)
    r = _run(nc, [arrays], core_ids=[0])
    return r.results[0]["out_0_dram"]
```

```python
from contextlib import ExitStack

import concourse.bass as bass
from concourse import mybir

F32 = mybir.dt.float32
F32R = mybir.dt.float32r
U32 = mybir.dt.uint32
ALU = mybir.AluOpType
ACT = mybir.ActivationFunctionType
AX_X = mybir.AxisListType.X

P = 128
EPS = 1e-5
VEC = ["L0_attn_ln0_g", "L0_attn_ln0_b", "L0_attn_ln1_g", "L0_attn_ln1_b", "L0_attn_time_decay",
       "L0_attn_time_first", "L0_attn_tm_k", "L0_attn_tm_v", "L0_attn_tm_r", "L0_attn_cm_k",
       "L0_attn_cm_r", "L0_ffn_ln1_g", "L0_ffn_ln1_b", "L0_ffn_ln2_g", "L0_ffn_ln2_b"]
SQUARE = ["L0_attn_Wk", "L0_attn_Wv", "L0_attn_Wr", "L0_attn_Wo", "L0_attn_Wcr",
          "L0_ffn_Wq", "L0_ffn_Wk", "L0_ffn_Wv", "L0_ffn_Wo"]


class Signal:

    def __init__(self, handle, per, start):
        self.sem, self.per, self.start = handle, per, start

    def at(self, b, k):
        return b * self.per + (k + self.start)

    def due(self, b, k):
        return not isinstance(b, int) or self.at(b, k) > self.start


class Chain:

    def __init__(self, engine, handle, per):
        self.engine, self.sem, self.per = engine, handle, per

    def begin(self, b, k=0):
        self.b, self.k = b, k

    def step(self, instruction):
        self.k += 1
        instruction.then_inc(self.sem, 1)

    def wait(self):
        self.engine.wait_ge(self.sem, self.b * self.per + self.k)

    def link(self, instruction):
        self.step(instruction)
        self.wait()

    def end(self):
        assert self.k == self.per, (self.sem, self.k, self.per)


def build(nc, t, out):
    x = t["L0_attn_x"]
    B, T, C = x.shape
    NT = T // P
    F = t["L0_attn_Wck"].shape[1]
    NF = F // P
    E = t["L0_ffn_Wg"].shape[1]
    H, DH = 16, C // 16
    G = 4
    NG = H // G
    HW = P // G
    RS = 3 * DH
    RM = RS + 2
    SCALE = float(DH) ** -0.5
    NEG = -1e38
    assert C == P and T == 512 and E == 8 and NF == 4

    with ExitStack() as ctx:
        def sb(name, shape, dt=F32):
            return ctx.enter_context(nc.sbuf_tensor(name, shape, dt))

        def bank(name, shape):
            return ctx.enter_context(nc.psum_tensor(name, shape, F32))

        def sig(name, per=1, start=0):
            return Signal(ctx.enter_context(nc.semaphore(name)), per, start)

        def sem(name):
            return ctx.enter_context(nc.semaphore(name))

        sq = {n: sb(n, [P, C]) for n in SQUARE}
        wck = sb("wck", [P, F])
        wcv = sb("wcv", [P, NF, C])
        wg = sb("wg", [P, E])
        b2 = sb("b2", [E, C])
        w1h = sb("w1h", [P, E, F], F32R)
        w1l = sb("w1l", [P, E, F], F32R)
        w2 = sb("w2", [P, E, NF, C])
        NV = len(VEC)
        rows = sb("rows", [NV + E * NF, P])
        cols = sb("cols", [P, NV + E * NF])
        ident = sb("ident", [P, P])
        half = sb("half", [P, NT])
        iota = sb("iota", [P, E])
        idle = sb("idle", [P, 2, 16])
        idle_turn = [0, 0]
        idle_act = sb("idle_act", [P, 1])
        idle_dve = sb("idle_dve", [P, 1])
        wdec = sb("wdec", [P, 1])
        wrow = sb("wrow", [P, T])
        col = {n: cols[:, i:i + 1] for i, n in enumerate(VEC)}

        X = sb("X", [P, NT, C])
        Z0 = sb("Z0", [P, NT, C])
        ZA = sb("ZA", [P, NT, C])
        XA = sb("XA", [P, T + 1])
        D = sb("D", [P, T])
        MK = sb("MK", [P, T])
        MV = sb("MV", [P, T])
        MR = sb("MR", [P, T])
        K = sb("K", [P, T])
        V = sb("V", [P, T])
        R = sb("R", [P, T])
        PP = sb("PP", [P, T + 1])
        EE = sb("EE", [P, 4, T])
        EV = sb("EV", [P, T])
        AA = sb("AA", [P, T + 1])
        BB = sb("BB", [P, T + 1])
        N2 = K
        D1 = D
        DD = EV
        N1 = EV
        GT = MV
        Y1 = sb("Y1", [P, NT, C])
        KK = EE
        RT = Z0
        X1 = sb("X1", [P, NT, C])
        Z1 = sb("Z1", [P, NT, C])
        HT = sb("HT", [P, T])
        QA = sb("QA", [P, NT, H, HW])
        KA = sb("KA", [P, NT, H, HW])
        VA = sb("VA", [P, NT, H, HW])
        KT = sb("KT", [P, NG, T], F32R)
        Q1 = sb("Q1", [P, NG, T], F32R)
        stA = sb("stA", [P, NT, 6])
        mvA = sb("mvA", [P, NT, 2])
        rsA = sb("rsA", [P, 4, NT])
        stH = sb("stH", [P, NT, 6])
        mvH = sb("mvH", [P, NT, 2])
        rsH = sb("rsH", [P, 4, NT])

        NM = sb("NM", [P, NT, H])
        Q2 = sb("Q2", [P, 2, T], F32R)
        PT = sb("PT", [P, 2 * G, T])
        CT = sb("CT", [P, T])
        RD = sb("RD", [P, NT, G])
        CX = sb("CX", [P, NT, H, DH])
        Z1b = sb("Z1b", [P, NT, C])

        CXT = sb("CXT", [P, T])
        Y3 = sb("Y3", [P, NT, C])
        XZ = sb("XZ", [P, NT, C])
        RES = sb("RES", [P, NT, C])
        ZM = sb("ZM", [P, NT, C])
        MT = sb("MT", [P, T])
        MH = sb("MH", [P, T], F32R)
        ML = sb("ML", [P, T], F32R)
        H1 = sb("H1", [P, 2, NF, T])
        w1 = H1[:, :, :, :].rearrange("p a f t -> p (a f t)").rearrange("p (e f) -> p e f", e=E)
        stC = sb("stC", [P, NT, 6])
        mvC = sb("mvC", [P, NT, 2])
        rsC = sb("rsC", [P, 4, NT])
        EX = sb("EX", [P, NT, E])
        PR = sb("PR", [P, NT, E])
        M8 = sb("M8", [P, NT, 8])
        I8 = sb("I8", [P, NT, 8], U32)
        IF = sb("IF", [P, NT, 2])
        K0 = sb("K0", [P, NT, E])
        K1 = sb("K1", [P, NT, E])
        g1 = sb("g1", [P, NT])
        g2 = sb("g2", [P, NT])
        WT = sb("WT", [P, NT, E])
        WTT = CXT[0:E, :]

        psA = bank("psA", [P, T])
        psS = bank("psS", [P, 2, T])
        psT = bank("psT", [P, 2, T])
        psV = bank("psV", [P, T])
        psH = bank("psH", [P, T])
        psY = bank("psY", [P, T])

        s_vec = sem("s_vec")
        s_sq = sem("s_sq")
        s_w1 = sem("s_w1")
        s_w2 = sem("s_w2")
        s_ident = sem("s_ident")
        s_const = sem("s_const")
        s_colT = sem("s_colT")
        s_cols = sem("s_cols")
        s_dec = sem("s_dec")
        s_wrow = sem("s_wrow")
        s_w1s = sem("s_w1s")

        USES = ["wo", "xc"] + [f"kk{f}" for f in range(NF)] + ["rr", "kv", "zh", "q", "k", "ZA", "kt0", "qt0",
                "kt1", "qt1", "K", "V", "R", "kt2", "qt2", "kt3", "qt3", "v"]
        HEAD_USES = [u for u in USES if u.isupper()]

        def use(b, name):
            if name in HEAD_USES:
                if isinstance(b, int) and b == 0:
                    return HEAD_USES.index(name)
                return b * len(USES) + (len(HEAD_USES) - len(USES) + USES.index(name))
            at = USES.index(name)
            if isinstance(b, int) and b == B - 1:
                at -= sum(u in HEAD_USES for u in USES[:at])
            return b * len(USES) + (len(HEAD_USES) + at)

        a_full = sem("a_full")
        a_taken = sem("a_taken")
        x_in = sig("x_in", 16)
        x_used = sig("x_used")
        h_stats = sig("h_stats")
        h_rstd = sig("h_rstd")
        zh_ready = sig("zh_ready")
        hd_ready = sig("hd_ready")
        hmix_ready = sig("hmix_ready", 3)
        a_stats = sig("a_stats", 2)
        a_rstd = sig("a_rstd", 2)
        za_ready = sig("za_ready", 2)
        d_ready = sig("d_ready")
        mix_ready = sig("mix_ready", 2)
        args_ready = sig("args_ready")
        exps_ready = sig("exps_ready")
        r_ready = sig("r_ready")
        n2_ready = sig("n2_ready")
        g_ready = sig("g_ready")
        kk_ready = sig("kk_ready", NF)
        z1_ready = sig("z1_ready")
        hi_ready = sig("hi_ready", 2)
        hi_copied = sig("hi_copied", 2)

        NS, NX = NG * NT * G, NG * (NT * G + 1)
        s_full = sig("s_full", NS)
        s_taken = sig("s_taken", NS)
        t_full = sig("t_full", NX)
        t_taken = sig("t_taken", NX)
        m_ready = sig("m_ready", NG)
        v_full = sig("v_full", NG * NT)
        c_full = sig("c_full", NG)
        ct_ready = sig("ct_ready", NG)
        cx_ready = sig("cx_ready", NG)
        kept = sig("kept")

        NH, NY = 3 + E * NF, 3 + E
        H_GATE = 2 + 2 * NF
        h_full = sig("h_full", NH)
        h_taken = sig("h_taken", NH, start=1)
        y_full = sig("y_full", NY)
        y_taken = sig("y_taken", NY, start=1)

        def h_use(e, f):
            return 2 + e * NF + f + (e >= 2)

        c_stats = sig("c_stats")
        c_rstd = sig("c_rstd")
        zm_ready = sig("zm_ready")
        ml_ready = sig("ml_ready")
        ex_ready = sig("ex_ready")
        wt_ready = sig("wt_ready")
        out_done = sig("out_done", 16, start=16)

        dve_h, dve_a, dve_c = sem("dve_h"), sem("dve_a"), sem("dve_c")
        dve_m, dve_x = sem("dve_m"), sem("dve_x")
        pool_h, pool_a, pool_c = sem("pool_h"), sem("pool_a"), sem("pool_c")

        def chunk(ap, c):
            return ap[:, c * P:(c + 1) * P]

        def heads(ap):
            return ap.rearrange("p (c h d) -> p c h d", h=H, d=DH)

        def tokens(ap):
            return ap.rearrange("p (c n) -> p c n", c=NT)

        def apart(engine):
            i = int(engine is nc.gpsimd)
            idle_turn[i] = (idle_turn[i] + 1) % 16
            unread = idle[:, i, idle_turn[i]:idle_turn[i] + 1]
            if engine is nc.gpsimd:
                engine.tensor_tensor(unread, half[:, 0:1], half[:, 0:1], ALU.mult)
            else:
                engine.tensor_copy(unread, half[:, 0:1])

        def over(engine, turn):
            turn(None, 0, None, None, slots=range(FIRST_HEAD, SLOTS))
            turn(0, 1, None, None)
            turn(1, 2, 0, None)
            with engine.Fori(2, B - 1) as n:
                turn(n, n + 1, n - 1, n - 2)
            turn(B - 1, None, B - 2, B - 3)
            turn(None, None, B - 1, B - 2)
            turn(None, None, None, B - 1)

        SLOTS, PER = 8 * NG, 8
        FIRST_HEAD = 20

        def extras(s, *parts):
            for b, table in parts:
                if b is not None:
                    for step in table.get(s, ()):
                        step(b)

        block = ctx.enter_context(nc.Block())

        @block.sync
        def _(sp):
            for i, n in enumerate(VEC):
                sp.dma_start(rows[i:i + 1, :], t[n].rearrange("(a n) -> a n", a=1)).then_inc(s_vec, 16)
            sp.dma_start(rows[NV:NV + E * NF, :],
                         t["L0_ffn_b1"].rearrange("e (c p) -> (e c) p", p=P)).then_inc(s_vec, 16)

            def load(b):
                if x_used.due(b, 0):
                    sp.wait_ge(x_used.sem, x_used.at(b, 0))
                sp.dma_start(X[:, :, :], x[b].rearrange("(c p) n -> p c n", p=P)).then_inc(x_in.sem, 16)

            def store(b):
                sp.wait_ge(y_taken.sem, y_taken.at(b, NY))
                sp.dma_start(out[b].rearrange("(c p) n -> p c n", p=P), RES[:, :, :]).then_inc(out_done.sem, 16)

            sp.sem_inc(out_done.sem, 16)
            load(0)
            for n in SQUARE:
                sp.dma_start(sq[n][:, :], t[n]).then_inc(s_sq, 16)
            sp.dma_start(wck[:, :], t["L0_attn_Wck"]).then_inc(s_sq, 16)
            sp.dma_start(wcv[:, :, :], t["L0_attn_Wcv"].rearrange("(c p) n -> p c n", p=P)).then_inc(s_sq, 16)
            sp.dma_start(wg[:, :], t["L0_ffn_Wg"]).then_inc(s_sq, 16)
            sp.dma_start(b2[:, :], t["L0_ffn_b2"]).then_inc(s_sq, 16)
            sp.dma_start(w1, t["L0_ffn_W1"].rearrange("e p f -> p e f")).then_inc(s_w1, 16)
            sp.dma_start(w2[:, :, :, :], t["L0_ffn_W2"].rearrange("e (c p) n -> p e c n", p=P)).then_inc(s_w2, 16)
            load(1)
            load(2)
            with sp.Fori(2, B - 1) as n:
                load(n + 1)
                store(n - 2)
            for b in range(B - 3, B):
                store(b)
            sp.wait_ge(out_done.sem, out_done.at(B - 1, 16))

        N_VEC, N_SQ, N_CONST = 16 * (NV + 1), 16 * (len(SQUARE) + 4), 10 + E

        @block.gpsimd
        def _(pool):
            pool.memset(ident[:, :], 0.0).then_inc(s_ident, 1)
            pool.wait_ge(s_ident, 1)
            pool.affine_select(out=ident[:, :], in_=ident[:, :], compare_op=ALU.not_equal, fill=1.0, base=0,
                               pattern=[[-1, P]], channel_multiplier=1).then_inc(s_ident, 1)
            pool.memset(half[:, :], -0.5).then_inc(s_const, 1)
            for e in range(E):
                pool.memset(iota[:, e:e + 1], float(e)).then_inc(s_const, 1)
            pool.memset(XA[:, 0:1], 0.0).then_inc(s_const, 1)
            pool.memset(PP[:, 0:1], NEG).then_inc(s_const, 1)
            pool.memset(AA[:, 0:1], 0.0).then_inc(s_const, 1)
            pool.memset(BB[:, 0:1], 0.0).then_inc(s_const, 1)
            pool.memset(QA[:, :, :, RS:HW], 0.0).then_inc(s_const, 1)
            pool.memset(KA[:, :, :, RM:HW], 0.0).then_inc(s_const, 1)
            pool.memset(KA[:, :, :, RS:RM], 1.0).then_inc(s_const, 1)
            pool.memset(VA[:, :, :, DH + 1:HW], 0.0).then_inc(s_const, 1)
            pool.memset(VA[:, :, :, DH:DH + 1], 1.0).then_inc(s_const, 1)
            pool.wait_ge(s_const, N_CONST)

            own_h = Chain(pool, pool_h, 6)
            own_a = Chain(pool, pool_a, 7)
            own_c = Chain(pool, pool_c, 1)

            def rstd(own, mv, rs, both):
                var = mv[:, :, 1]
                own.link(pool.tensor_scalar(rs[:, 1, :], var, EPS, None, ALU.add))
                last = pool.tensor_tensor(rs[:, 0, :], rs[:, 1, :], half[:, :], ALU.pow)
                if not both:
                    return last
                own.link(last)
                own.link(pool.tensor_tensor(rs[:, 1, :], rs[:, 0, :], rs[:, 0, :], ALU.mult))
                own.step(pool.tensor_tensor(rs[:, 1, :], rs[:, 1, :], var, ALU.mult))
                own.wait()
                apart(pool)
                own.link(pool.tensor_scalar(rs[:, 1, :], rs[:, 1, :], EPS, None, ALU.add))
                own.link(pool.tensor_tensor(rs[:, 2, :], rs[:, 1, :], half[:, :], ALU.pow))
                return pool.tensor_tensor(rs[:, 3, :], rs[:, 2, :], rs[:, 0, :], ALU.mult)

            def shift(b, u):
                pool.wait_ge(a_taken, use(b, u) + 1)
                return pool.tensor_tensor(D[:, :], XA[:, 1:T + 1], XA[:, 0:T], ALU.subtract)

            def head_norm(b):
                own_h.begin(b)
                pool.wait_ge(h_stats.sem, h_stats.at(b, 1))
                apart(pool)
                rstd(own_h, mvH, rsH, True).then_inc(h_rstd.sem, 1)
                own_h.end()

            def head_shift(b):
                shift(b, "ZA").then_inc(hd_ready.sem, 1)

            def head_sigmoid(b):
                pool.wait_ge(a_taken, use(b, "R") + 1)
                apart(pool)
                pool.tensor_scalar(R[:, :], R[:, :], 0.5, 0.5, ALU.mult, ALU.add).then_inc(r_ready.sem, 1)

            def side(b):
                pool.wait_ge(exps_ready.sem, exps_ready.at(b, 1))
                pool.tensor_tensor(N2[:, :], EE[:, 3, :], V[:, :], ALU.mult).then_inc(n2_ready.sem, 1)

            def norm_1(b):
                own_a.begin(b)
                pool.wait_ge(a_stats.sem, a_stats.at(b, 1))
                apart(pool)
                rstd(own_a, mvA, rsA, False).then_inc(a_rstd.sem, 1)

            def tail_shift(b):
                shift(b, "xc").then_inc(d_ready.sem, 1)

            def square(b):
                for f in range(NF):
                    pool.wait_ge(a_taken, use(b, f"kk{f}") + 1)
                    pool.tensor_tensor(KK[:, f, :], KK[:, f, :], KK[:, f, :], ALU.mult).then_inc(kk_ready.sem, 1)

            def norm_2(b):
                pool.wait_ge(a_stats.sem, a_stats.at(b, 2))
                apart(pool)
                rstd(own_a, mvA, rsA, True).then_inc(a_rstd.sem, 1)
                own_a.end()

            def copy_hi(b):
                pool.wait_ge(hi_ready.sem, hi_ready.at(b, 1))
                apart(pool)
                pool.tensor_copy(QA[:, :, :, DH:2 * DH], QA[:, :, :, 0:DH]).then_inc(hi_copied.sem, 1)
                pool.wait_ge(hi_ready.sem, hi_ready.at(b, 2))
                apart(pool)
                pool.tensor_copy(KA[:, :, :, 2 * DH:RS], KA[:, :, :, 0:DH]).then_inc(hi_copied.sem, 1)

            def keep(b):
                pool.wait_ge(z1_ready.sem, z1_ready.at(b, 1))
                if y_taken.due(b - 1, 1):
                    pool.wait_ge(y_taken.sem, y_taken.at(b - 1, 1))
                pool.tensor_tensor(XZ[:, :, :], X1[:, :, :], Z1[:, :, :], ALU.add)
                pool.tensor_scalar(Z1b[:, :, :], Z1[:, :, :], 1.0, None, ALU.mult).then_inc(kept.sem, 1)

            def c_norm(b):
                own_c.begin(b)
                pool.wait_ge(c_stats.sem, c_stats.at(b, 1))
                apart(pool)
                rstd(own_c, mvC, rsC, False).then_inc(c_rstd.sem, 1)
                own_c.end()

            def c_split(b):
                pool.wait_ge(h_taken.sem, h_taken.at(b, 2))
                pool.tensor_tensor(ML[:, :], MT[:, :], MH[:, :].bitcast(F32), ALU.subtract).then_inc(ml_ready.sem, 1)

            HEAD = {20: (head_norm,), 24: (head_shift,), 27: (head_sigmoid,)}
            TAIL = {4: (side,), 8: (norm_1,), 10: (tail_shift,), 13: (square,), 17: (norm_2,), 22: (copy_hi,)}
            CORE = {6: (keep,)}
            POST = {2: (c_norm,), 4: (c_split,)}

            def turn(tail, head, core, post, slots=range(SLOTS)):
                for s in slots:
                    extras(s, (post, POST), (core, CORE), (tail, TAIL), (head, HEAD))

            over(pool, turn)

        @block.scalar
        def _(act):
            act.wait_ge(s_colT, 1)
            act.activation(cols[:, :], psA[:, 0:NV + E * NF], ACT.Copy).then_inc(s_cols, 1)
            act.wait_ge(s_cols, 1)
            act.activation(wdec[:, :], col["L0_attn_time_decay"], ACT.Exp).then_inc(s_dec, 1)
            act.wait_ge(s_const, N_CONST)
            act.activation(idle_act[:, :], half[:, 0:1], ACT.Copy).then_inc(h_taken.sem, 1)

            def affine(dst, src, g, c):
                return act.activation(dst, src, ACT.Identity, bias=col[c], scale=col[g])

            def head_rows(b):
                act.wait_ge(a_full, use(b, "ZA") + 1)
                affine(XA[:, 1:T + 1], psA[:, :], "L0_attn_ln0_g", "L0_attn_ln0_b").then_inc(a_taken, 1)

            def head_kv(b):
                act.wait_ge(a_full, use(b, "K") + 1)
                act.activation(K[:, :], psA[:, :], ACT.Copy).then_inc(a_taken, 1)
                act.wait_ge(a_full, use(b, "V") + 1)
                act.activation(V[:, :], psA[:, :], ACT.Copy).then_inc(a_taken, 1)
                act.wait_ge(a_full, use(b, "R") + 1)
                act.activation(R[:, :], psA[:, :], ACT.Tanh, scale=0.5).then_inc(a_taken, 1)

            def wkv_exps(b):
                act.wait_ge(args_ready.sem, args_ready.at(b, 1))
                act.activation(EE[:, :, :], EE[:, :, :], ACT.Exp).then_inc(exps_ready.sem, 1)

            def rows_1(b):
                act.wait_ge(a_full, use(b, "xc") + 1)
                affine(XA[:, 1:T + 1], psA[:, :], "L0_attn_ln1_g", "L0_attn_ln1_b").then_inc(a_taken, 1)

            def relu(f):
                def step(b):
                    act.wait_ge(a_full, use(b, f"kk{f}") + 1)
                    act.activation(KK[:, f, :], psA[:, :], ACT.Relu).then_inc(a_taken, 1)
                return step

            def receptance(b):
                act.wait_ge(a_full, use(b, "rr") + 1)
                act.activation(RT[:, :, :], tokens(psA[:, :]), ACT.Tanh, scale=0.5).then_inc(a_taken, 1)

            def rows_2(b):
                act.wait_ge(a_full, use(b, "zh") + 1)
                affine(HT[:, :], psA[:, :], "L0_ffn_ln1_g", "L0_ffn_ln1_b").then_inc(a_taken, 1)

            def take_kt(g):
                def step(b):
                    act.wait_ge(a_full, use(b, f"kt{g}") + 1)
                    act.activation(KT[:, g, :], psA[:, :], ACT.Copy).then_inc(a_taken, 1)
                return step

            def take_v(b):
                if v_full.due(b, 0):
                    act.wait_ge(v_full.sem, v_full.at(b, 0))
                act.wait_ge(a_full, use(b, "v") + 1)
                act.activation(VA[:, :, :, 0:DH], heads(psA[:, :]), ACT.Copy).then_inc(a_taken, 1)

            def q2(b, g):
                n = g * (NT * G + 1)
                act.wait_ge(t_full.sem, t_full.at(b, n + 1))
                act.activation(Q2[:, g % 2, :], psT[:, n % 2, :], ACT.Copy).then_inc(t_taken.sem, 1)

            def exps(b, g, c):
                for j in range(G):
                    n = g * (NT * G + 1) + 1 + c * G + j
                    if j == 0:
                        if v_full.due(b, g * NT + c - 1):
                            act.wait_ge(v_full.sem, v_full.at(b, g * NT + c - 1))
                    act.wait_ge(t_full.sem, t_full.at(b, n + 1))
                    act.activation(PT[:, (c % 2) * G + j, :], psT[:, n % 2, :], ACT.Exp,
                                   scale=SCALE).then_inc(t_taken.sem, 1)

            def c_ctx(b):
                act.wait_ge(h_full.sem, h_full.at(b, 1))
                act.activation(CXT[:, :], psH[:, :], ACT.Copy).then_inc(h_taken.sem, 1)

            def c_norm(b):
                act.wait_ge(h_full.sem, h_full.at(b, 2))
                affine(MH[:, :], psH[:, :], "L0_ffn_ln2_g", "L0_ffn_ln2_b")
                affine(MT[:, :], psH[:, :], "L0_ffn_ln2_g", "L0_ffn_ln2_b").then_inc(h_taken.sem, 1)

            def c_gate(b):
                act.wait_ge(y_taken.sem, y_taken.at(b, 2))
                act.activation(EX[:, :, :], EX[:, :, :], ACT.Exp).then_inc(ex_ready.sem, 1)

            def c_gate_t(b):
                act.wait_ge(h_full.sem, h_full.at(b, H_GATE + 1))
                act.activation(WTT, psH[0:E, :], ACT.Copy).then_inc(h_taken.sem, 1)

            def gelu(b, e, f):
                if e >= 2 and f == 0:
                    act.wait_ge(y_full.sem, y_full.at(b, 2 + e - 1))
                act.wait_ge(h_full.sem, h_full.at(b, h_use(e, f) + 1))
                act.activation(H1[:, e % 2, f, :], psH[:, :], ACT.Gelu_apprx_tanh,
                               bias=cols[:, NV + e * NF + f:NV + e * NF + f + 1]).then_inc(h_taken.sem, 1)

            HEAD = {23: (head_rows,), 26: (head_kv,)}
            TAIL = {0: (wkv_exps,), 10: (rows_1,), 13: (relu(0), relu(1)), 14: (relu(2), relu(3)), 15: (receptance,),
                    20: (rows_2,), 23: (take_kt(0),), 25: (take_kt(1),), 27: (take_kt(2),), 28: (take_kt(3), take_v)}
            POST = {0: (c_ctx,), 3: (c_norm,), 8: (c_gate,), 12: (c_gate_t,)}

            def turn(tail, head, core, post, slots=range(SLOTS)):
                for s in slots:
                    g, k = divmod(s, PER)
                    extras(s, (post, POST), (head, HEAD), (tail, TAIL))
                    if k < NT and core is not None:
                        exps(core, g, k)
                    if k == 6:
                        nxt = core if g + 1 < NG else tail
                        if nxt is not None:
                            q2(nxt, (g + 1) % NG)
                    if k >= NT and post is not None:
                        e, f = 2 * g + (k - NT) // 2, (k - NT) % 2 * 2
                        gelu(post, e, f)
                        gelu(post, e, f + 1)

            over(act, turn)

        @block.tensor
        def _(pe):
            pe.wait_ge(s_ident, 2)
            pe.wait_ge(s_vec, N_VEC)
            pe.transpose(psA[:, 0:NV + E * NF], rows[:, :], ident[0:NV + E * NF, 0:NV + E * NF]).then_inc(s_colT, 1)
            pe.wait_ge(s_cols, 1)
            pe.wait_ge(s_const, N_CONST)
            pe.wait_ge(s_sq, N_SQ)

            def transposes(dst, src):
                for c in range(NT):
                    last = pe.transpose(chunk(dst, c), src[:, c, :], ident[:, :])
                return last

            def to_tokens(dst, src, w):
                for c in range(NT):
                    last = pe.matmul(chunk(dst, c), chunk(src, c), w, start=True, stop=True)
                return last

            def head_rows(b):
                pe.wait_ge(zh_ready.sem, zh_ready.at(b, 1))
                if not isinstance(b, int) or b > 0:
                    pe.wait_ge(a_taken, use(b, "ZA"))
                transposes(psA, ZA).then_inc(a_full, 1)

            def head_kv(b):
                for i, (u, n, m) in enumerate((("K", "L0_attn_Wk", MK), ("V", "L0_attn_Wv", MV), ("R", "L0_attn_Wr", MR))):
                    pe.wait_ge(hmix_ready.sem, hmix_ready.at(b, i + 1))
                    pe.wait_ge(a_taken, use(b, u))
                    pe.matmul(psA[:, :], sq[n][:, :], m[:, :], start=True, stop=True).then_inc(a_full, 1)

            def time_mix_out(b):
                pe.wait_ge(g_ready.sem, g_ready.at(b, 1))
                pe.wait_ge(a_taken, use(b, "wo"))
                to_tokens(psA, GT, sq["L0_attn_Wo"][:, :]).then_inc(a_full, 1)

            def rows_1(b):
                pe.wait_ge(za_ready.sem, za_ready.at(b, 1))
                pe.wait_ge(a_taken, use(b, "xc"))
                transposes(psA, ZA).then_inc(a_full, 1)

            def channel_mix_in(f):
                def step(b):
                    if f == 0:
                        pe.wait_ge(mix_ready.sem, mix_ready.at(b, 1))
                    pe.wait_ge(a_taken, use(b, f"kk{f}"))
                    pe.matmul(psA[:, :], chunk(wck, f), MK[:, :], start=True, stop=True).then_inc(a_full, 1)
                return step

            def receptance(b):
                pe.wait_ge(mix_ready.sem, mix_ready.at(b, 2))
                pe.wait_ge(a_taken, use(b, "rr"))
                to_tokens(psA, MR, sq["L0_attn_Wcr"][:, :]).then_inc(a_full, 1)

            def channel_mix_out():
                for c in range(NT):
                    for f in range(NF):
                        last = pe.matmul(chunk(psA, c), chunk(KK[:, f, :], c), wcv[:, f, :],
                                         start=(f == 0), stop=(f == NF - 1))
                return last

            def channel_mix(b):
                pe.wait_ge(kk_ready.sem, kk_ready.at(b, NF))
                pe.wait_ge(a_taken, use(b, "kv"))
                channel_mix_out().then_inc(a_full, 1)

            def rows_2(b):
                pe.wait_ge(za_ready.sem, za_ready.at(b, 2))
                pe.wait_ge(a_taken, use(b, "zh"))
                transposes(psA, ZA).then_inc(a_full, 1)

            def project_qk(b):
                pe.wait_ge(a_taken, use(b, "zh") + 1)
                for u, n in (("q", "L0_ffn_Wq"), ("k", "L0_ffn_Wk")):
                    pe.wait_ge(a_taken, use(b, u))
                    to_tokens(psA, HT, sq[n][:, :]).then_inc(a_full, 1)

            def project_v(b):
                pe.wait_ge(a_taken, use(b, "v"))
                to_tokens(psA, HT, sq["L0_ffn_Wv"][:, :]).then_inc(a_full, 1)

            def turn_qk(g):
                def step(b):
                    if g == 0:
                        pe.wait_ge(hi_copied.sem, hi_copied.at(b, 2))
                    for u, parts in ((f"kt{g}", KA), (f"qt{g}", QA)):
                        pe.wait_ge(a_taken, use(b, u))
                        transposes(psA, parts[:, :, g * G:(g + 1) * G, :].rearrange("p c h w -> p c (h w)")).then_inc(a_full, 1)
                return step

            def scores(b, g, c):
                if c == 0:
                    pe.wait_ge(a_taken, use(b, f"qt{g}") + 1)
                for j in range(G):
                    n = (g * NT + c) * G + j
                    if s_taken.due(b, n - 1):
                        pe.wait_ge(s_taken.sem, s_taken.at(b, n - 1))
                    r = slice(j * HW, j * HW + RS)
                    pe.matmul(psS[:, n % 2, :], chunk(Q1[r, g, :], c), KT[r, g, :],
                              start=True, stop=True).then_inc(s_full.sem, 1)

            def q2(b, g):
                n = g * (NT * G + 1)
                pe.wait_ge(m_ready.sem, m_ready.at(b, g + 1))
                if t_taken.due(b, n - 1):
                    pe.wait_ge(t_taken.sem, t_taken.at(b, n - 1))
                transposes(psT[:, n % 2, :], QA[:, :, g * G:(g + 1) * G, :].rearrange(
                    "p c h w -> p c (h w)")).then_inc(t_full.sem, 1)

            def scores_t(b, g, c):
                if c == 0:
                    pe.wait_ge(t_taken.sem, t_taken.at(b, g * (NT * G + 1) + 1))
                for j in range(G):
                    n = g * (NT * G + 1) + 1 + c * G + j
                    if t_taken.due(b, n - 1):
                        pe.wait_ge(t_taken.sem, t_taken.at(b, n - 1))
                    r = slice(j * HW, j * HW + RM)
                    pe.matmul(psT[:, n % 2, :], chunk(KT[r, g, :], c), Q2[r, g % 2, :],
                              start=True, stop=True).then_inc(t_full.sem, 1)

            def times_v(b, g, c):
                pe.wait_ge(t_taken.sem, t_taken.at(b, g * (NT * G + 1) + 1 + (c + 1) * G))
                if c == 0:
                    if cx_ready.due(b, g):
                        pe.wait_ge(cx_ready.sem, cx_ready.at(b, g))
                for j in range(G):
                    r = slice(j * HW, (j + 1) * HW)
                    last = pe.matmul(psV[r, :], VA[:, c, g * G + j, :], PT[:, (c % 2) * G + j, :],
                                     start=(c == 0), stop=(c == NT - 1))
                last.then_inc(v_full.sem, 1)

            def context(b, g):
                pe.wait_ge(ct_ready.sem, ct_ready.at(b, g + 1))
                for c in range(NT):
                    last = pe.transpose(chunk(psV, c), chunk(CT, c), ident[:, :])
                last.then_inc(c_full.sem, 1)

            def c_ctx(b):
                pe.wait_ge(cx_ready.sem, cx_ready.at(b, NG))
                if h_taken.due(b, 0):
                    pe.wait_ge(h_taken.sem, h_taken.at(b, 0))
                transposes(psH, CX[:, :, :, :].rearrange("p c h d -> p c (h d)")).then_inc(h_full.sem, 1)

            def c_out(b):
                pe.wait_ge(h_taken.sem, h_taken.at(b, 1))
                if y_taken.due(b, 0):
                    pe.wait_ge(y_taken.sem, y_taken.at(b, 0))
                to_tokens(psY, CXT, sq["L0_ffn_Wo"][:, :]).then_inc(y_full.sem, 1)

            def c_norm(b):
                pe.wait_ge(zm_ready.sem, zm_ready.at(b, 1))
                transposes(psH, ZM).then_inc(h_full.sem, 1)

            def c_logits(b):
                pe.wait_ge(h_taken.sem, h_taken.at(b, 2))
                pe.wait_ge(y_taken.sem, y_taken.at(b, 1))
                for c in range(NT):
                    last = pe.matmul(psY[:, c * E:(c + 1) * E], chunk(MT, c), wg[:, :], start=True, stop=True)
                last.then_inc(y_full.sem, 1)

            def c_gate(b):
                pe.wait_ge(wt_ready.sem, wt_ready.at(b, 1))
                pe.wait_ge(h_taken.sem, h_taken.at(b, H_GATE))
                for c in range(NT):
                    last = pe.transpose(chunk(psH[0:E, :], c), WT[:, c, :], ident[:, :])
                last.then_inc(h_full.sem, 1)

            def c_bias(b):
                pe.wait_ge(h_taken.sem, h_taken.at(b, H_GATE + 1))
                pe.wait_ge(y_taken.sem, y_taken.at(b, 2 + E))
                to_tokens(psY, WTT, b2[:, :]).then_inc(y_full.sem, 1)

            def hidden(b, e, f):
                if e == 0 and f == 0:
                    pe.wait_ge(ml_ready.sem, ml_ready.at(b, 1))
                    pe.wait_ge(s_w1s, 1)
                pe.wait_ge(h_taken.sem, h_taken.at(b, h_use(e, f)))
                w = slice(f * P, (f + 1) * P)
                pe.matmul(psH[:, :], w1h[:, e, w], MH[:, :], start=True, stop=False)
                pe.matmul(psH[:, :], w1h[:, e, w], ML[:, :], start=False, stop=False)
                pe.matmul(psH[:, :], w1l[:, e, w], MH[:, :], start=False, stop=True).then_inc(h_full.sem, 1)

            def expert(b, e, c):
                if c == 0:
                    pe.wait_ge(s_w2, 16)
                    pe.wait_ge(h_taken.sem, h_taken.at(b, h_use(e, NF - 1) + 1))
                    pe.wait_ge(y_taken.sem, y_taken.at(b, 2 + e))
                for f in range(NF):
                    last = pe.matmul(chunk(psY, c), chunk(H1[:, e % 2, f, :], c), w2[:, e, f, :],
                                     start=(f == 0), stop=(f == NF - 1))
                if c == NT - 1:
                    last.then_inc(y_full.sem, 1)

            HEAD = {23: (head_rows,), 26: (head_kv,)}
            TAIL = {7: (time_mix_out,), 10: (rows_1,), 13: (channel_mix_in(0), channel_mix_in(1)),
                    14: (channel_mix_in(2), channel_mix_in(3)), 15: (receptance,), 16: (channel_mix,), 20: (rows_2,),
                    22: (project_qk,), 23: (turn_qk(0),), 25: (turn_qk(1),), 27: (turn_qk(2),),
                    28: (turn_qk(3), project_v)}
            POST = {0: (c_ctx,), 1: (c_out,), 3: (c_norm,), 4: (c_logits,), 11: (c_gate,)}

            def turn(tail, head, core, post, slots=range(SLOTS)):
                for s in slots:
                    g, k = divmod(s, PER)
                    nxt = core if g + 1 < NG else tail
                    extras(s, (post, POST), (head, HEAD), (tail, TAIL))
                    if k < NT:
                        if nxt is not None:
                            scores(nxt, (g + 1) % NG, k)
                        if core is not None:
                            scores_t(core, g, k)
                            if k:
                                times_v(core, g, k - 1)
                    if k == NT and core is not None:
                        times_v(core, g, NT - 1)
                    if k == 5 and nxt is not None:
                        q2(nxt, (g + 1) % NG)
                    if k == 5 and core is not None:
                        context(core, g)
                    if k >= NT and post is not None:
                        for i in range(2):
                            e, f = 2 * g + (k - NT) // 2, (k - NT) % 2 * 2 + i
                            hidden(post, e, f)
                            if e:
                                expert(post, e - 1, f)
                if post is not None:
                    for c in range(NT):
                        expert(post, E - 1, c)
                    c_bias(post)

            over(pe, turn)

        @block.vector
        def _(dve):
            own_h = Chain(dve, dve_h, 3)
            own_a = Chain(dve, dve_a, 11)
            own_m = Chain(dve, dve_m, NG)
            own_x = Chain(dve, dve_x, NG)
            own_c = Chain(dve, dve_c, 14)
            dve.wait_ge(s_dec, 1)
            dve.tensor_scalar(wdec[:, :], wdec[:, :], -1.0, None, ALU.mult).then_inc(s_wrow, 1)
            dve.memset(wrow[:, :], 0.0).then_inc(s_wrow, 1)
            dve.wait_ge(s_wrow, 2)
            dve.tensor_scalar(wrow[:, :], wrow[:, :], wdec[:, 0:1], None, ALU.add).then_inc(s_wrow, 1)
            dve.wait_ge(s_wrow, 3)
            dve.wait_ge(s_const, N_CONST)
            dve.tensor_copy(idle_dve[:, :], half[:, 0:1]).then_inc(y_taken.sem, 1)

            def split_w1():
                dve.wait_ge(s_w1, 16)
                dve.tensor_copy(w1h[:, :, :], w1).then_inc(s_wrow, 1)
                dve.wait_ge(s_wrow, 4)
                dve.tensor_tensor(w1l[:, :, :], w1, w1h[:, :, :].bitcast(F32), ALU.subtract).then_inc(s_w1s, 1)

            def stats(own, src, st, mv):
                for c in range(NT):
                    last = dve.bn_stats(st[:, c, :], src[:, c, :])
                own.step(last)
                own.wait()
                apart(dve)
                for c in range(NT):
                    last = dve.bn_aggr(mv[:, c, :], st[:, c, :])
                return last

            def normed(dst, src, mv, rs):
                for c in range(NT):
                    last = dve.tensor_scalar(dst[:, c, :], src[:, c, :], mv[:, c, 0:1], rs[:, c:c + 1],
                                             ALU.subtract, ALU.mult)
                return last

            def mix(dst, name):
                return dve.scalar_tensor_tensor(out=dst[:, :], in0=D[:, :], scalar=col[name], in1=XA[:, 0:T],
                                                op0=ALU.mult, op1=ALU.add)

            def head_stats(b):
                own_h.begin(b)
                dve.wait_ge(x_in.sem, x_in.at(b, 16))
                stats(own_h, X, stH, mvH).then_inc(h_stats.sem, 1)

            def head_norm(b):
                dve.wait_ge(h_rstd.sem, h_rstd.at(b, 1))
                normed(ZA, X, mvH, rsH[:, 3, :]).then_inc(zh_ready.sem, 1)
                normed(Z0, X, mvH, rsH[:, 0, :])

            def head_mixes(b):
                dve.wait_ge(hd_ready.sem, hd_ready.at(b, 1))
                for m, n in ((MK, "L0_attn_tm_k"), (MV, "L0_attn_tm_v"), (MR, "L0_attn_tm_r")):
                    mix(m, n).then_inc(hmix_ready.sem, 1)

            def wkv_args(b):
                dve.wait_ge(a_taken, use(b, "K") + 1)
                own_h.link(dve.tensor_tensor_scan(PP[:, 1:T + 1], wrow[:, :], K[:, :], NEG, ALU.add, ALU.max))
                dve.scalar_tensor_tensor(out=EE[:, 0, :], in0=PP[:, 0:T], scalar=wdec[:, 0:1], in1=PP[:, 1:T + 1],
                                         op0=ALU.add, op1=ALU.subtract)
                dve.tensor_tensor(EE[:, 1, :], K[:, :], PP[:, 1:T + 1], ALU.subtract)
                own_h.link(dve.scalar_tensor_tensor(out=DD[:, :], in0=K[:, :], scalar=col["L0_attn_time_first"],
                                                    in1=PP[:, 0:T], op0=ALU.add, op1=ALU.subtract))
                dve.tensor_scalar(EE[:, 2, :], DD[:, :], 0.0, -1.0, ALU.max, ALU.mult)
                dve.tensor_scalar(EE[:, 3, :], DD[:, :], 0.0, None, ALU.min).then_inc(args_ready.sem, 1)
                own_h.end()

            def wkv_scans(b):
                own_a.begin(b)
                dve.wait_ge(exps_ready.sem, exps_ready.at(b, 1))
                dve.wait_ge(a_taken, use(b, "V") + 1)
                own_a.link(dve.tensor_tensor(EV[:, :], EE[:, 1, :], V[:, :], ALU.mult))
                dve.tensor_tensor_scan(BB[:, 1:T + 1], EE[:, 0, :], EE[:, 1, :], 0.0, ALU.mult, ALU.add)
                own_a.link(dve.tensor_tensor_scan(AA[:, 1:T + 1], EE[:, 0, :], EV[:, :], 0.0, ALU.mult, ALU.add))

            def wkv_out(b):
                dve.tensor_tensor(N1[:, :], EE[:, 2, :], AA[:, 0:T], ALU.mult)
                own_a.link(dve.tensor_tensor(D1[:, :], EE[:, 2, :], BB[:, 0:T], ALU.mult))
                own_a.link(dve.tensor_tensor(D1[:, :], D1[:, :], EE[:, 3, :], ALU.add))
                own_a.link(dve.reciprocal(D1[:, :], D1[:, :]))
                dve.wait_ge(n2_ready.sem, n2_ready.at(b, 1))
                own_a.link(dve.tensor_tensor(N1[:, :], N1[:, :], N2[:, :], ALU.add))
                own_a.link(dve.tensor_tensor(N1[:, :], N1[:, :], D1[:, :], ALU.mult))
                dve.wait_ge(r_ready.sem, r_ready.at(b, 1))
                dve.tensor_tensor(GT[:, :], N1[:, :], R[:, :], ALU.mult).then_inc(g_ready.sem, 1)

            def stats_1(b):
                dve.wait_ge(a_full, use(b, "wo") + 1)
                dve.tensor_tensor(Y1[:, :, :], tokens(psA[:, :]), Z0[:, :, :], ALU.add).then_inc(a_taken, 1)
                dve.wait_ge(a_taken, use(b, "wo") + 1)
                stats(own_a, Y1, stA, mvA).then_inc(a_stats.sem, 1)

            def norm_1(b):
                dve.wait_ge(a_rstd.sem, a_rstd.at(b, 1))
                normed(ZA, Y1, mvA, rsA[:, 0, :]).then_inc(za_ready.sem, 1)

            def mixes(b):
                dve.wait_ge(d_ready.sem, d_ready.at(b, 1))
                for m, n in ((MK, "L0_attn_cm_k"), (MR, "L0_attn_cm_r")):
                    mix(m, n).then_inc(mix_ready.sem, 1)

            def stats_2(b):
                dve.wait_ge(a_taken, use(b, "rr") + 1)
                own_a.link(dve.tensor_scalar(RT[:, :, :], RT[:, :, :], 0.5, 0.5, ALU.mult, ALU.add))
                dve.wait_ge(a_full, use(b, "kv") + 1)
                dve.tensor_tensor(RT[:, :, :], tokens(psA[:, :]), RT[:, :, :], ALU.mult).then_inc(a_taken, 1)
                own_a.link(dve.tensor_tensor(Y1[:, :, :], Y1[:, :, :], X[:, :, :], ALU.add))
                dve.wait_ge(a_taken, use(b, "kv") + 1)
                if kept.due(b, 0):
                    dve.wait_ge(kept.sem, kept.at(b, 0))
                dve.tensor_tensor(X1[:, :, :], RT[:, :, :], Y1[:, :, :], ALU.add).then_inc(x_used.sem, 1)
                dve.wait_ge(x_used.sem, x_used.at(b, 1))
                stats(own_a, X1, stA, mvA).then_inc(a_stats.sem, 1)
                own_a.end()

            def norm_2(b):
                dve.wait_ge(a_rstd.sem, a_rstd.at(b, 2))
                normed(ZA, X1, mvA, rsA[:, 3, :]).then_inc(za_ready.sem, 1)
                normed(Z1, X1, mvA, rsA[:, 0, :]).then_inc(z1_ready.sem, 1)

            def split_qk(b):
                if t_full.due(b - 1, (NG - 1) * (NT * G + 1) + 1):
                    dve.wait_ge(t_full.sem, t_full.at(b - 1, (NG - 1) * (NT * G + 1) + 1))
                for i, (u, parts, lo) in enumerate((("q", QA, 2 * DH), ("k", KA, DH))):
                    dve.wait_ge(a_full, use(b, u) + 1)
                    dve.tensor_copy(parts[:, :, :, 0:DH].bitcast(F32R), heads(psA[:, :])).then_inc(hi_ready.sem, 1)
                    dve.wait_ge(hi_ready.sem, hi_ready.at(b, i + 1))
                    dve.tensor_tensor(parts[:, :, :, lo:lo + DH], heads(psA[:, :]), parts[:, :, :, 0:DH],
                                      ALU.subtract).then_inc(a_taken, 1)

            def take_qt(g):
                def step(b):
                    dve.wait_ge(a_full, use(b, f"qt{g}") + 1)
                    dve.tensor_copy(Q1[:, g, :], psA[:, :]).then_inc(a_taken, 1)
                return step

            def maxima(b, g, c):
                for j in range(G):
                    n = (g * NT + c) * G + j
                    dve.wait_ge(s_full.sem, s_full.at(b, n + 1))
                    dve.tensor_reduce(NM[:, c, g * G + j:g * G + j + 1], psS[:, n % 2, :], AX_X, ALU.max,
                                      negate=True).then_inc(s_taken.sem, 1)
                if c == NT - 1:
                    own_m.begin(b, g)
                    dve.wait_ge(s_taken.sem, s_taken.at(b, (g + 1) * NT * G))
                    hs = slice(g * G, (g + 1) * G)
                    own_m.link(dve.tensor_copy(QA[:, :, hs, RS].bitcast(F32R), NM[:, :, hs]))
                    dve.tensor_tensor(QA[:, :, hs, RS + 1], NM[:, :, hs], QA[:, :, hs, RS],
                                      ALU.subtract).then_inc(m_ready.sem, 1)

            def context_t(b, g):
                dve.wait_ge(v_full.sem, v_full.at(b, (g + 1) * NT))
                dve.tensor_copy(CT[:, :], psV[:, :]).then_inc(ct_ready.sem, 1)

            def context(b, g):
                dve.wait_ge(c_full.sem, c_full.at(b, g + 1))
                if g == 0:
                    own_x.begin(b)
                    if h_full.due(b - 1, 1):
                        dve.wait_ge(h_full.sem, h_full.at(b - 1, 1))
                ctx4 = psV[:, :].rearrange("p (c j w) -> p c j w", c=NT, w=HW)
                own_x.link(dve.reciprocal(RD[:, :, :], ctx4[:, :, :, DH]))
                dve.tensor_tensor(CX[:, :, g * G:(g + 1) * G, :], ctx4[:, :, :, 0:DH],
                                  RD[:, :, :].unsqueeze(3).to_broadcast([P, NT, G, DH]), ALU.mult).then_inc(cx_ready.sem, 1)
                if g == NG - 1:
                    own_x.end()

            def c_ctx(b):
                own_c.begin(b)
                dve.wait_ge(kept.sem, kept.at(b, 1))
                if out_done.due(b, 0):
                    dve.wait_ge(out_done.sem, out_done.at(b, 0))
                dve.wait_ge(y_full.sem, y_full.at(b, 1))
                own_c.link(dve.tensor_tensor(Y3[:, :, :], tokens(psY[:, :]), Z1b[:, :, :], ALU.add))
                dve.tensor_tensor(RES[:, :, :], tokens(psY[:, :]), XZ[:, :, :], ALU.add).then_inc(y_taken.sem, 1)
                stats(own_c, Y3, stC, mvC).then_inc(c_stats.sem, 1)

            def c_norm(b):
                dve.wait_ge(c_rstd.sem, c_rstd.at(b, 1))
                normed(ZM, Y3, mvC, rsC[:, 0, :]).then_inc(zm_ready.sem, 1)

            def bc(v):
                return v.unsqueeze(2).to_broadcast([P, NT, E])

            def c_gate(b):
                dve.wait_ge(y_full.sem, y_full.at(b, 2))
                logits = psY[:, 0:NT * E].rearrange("p (c e) -> p c e", e=E)
                own_c.link(dve.tensor_reduce(g1[:, :], logits, AX_X, ALU.max))
                dve.tensor_tensor(EX[:, :, :], logits, bc(g1[:, :]), ALU.subtract).then_inc(y_taken.sem, 1)

            def c_top(b):
                dve.wait_ge(ex_ready.sem, ex_ready.at(b, 1))
                own_c.link(dve.tensor_reduce(g1[:, :], EX[:, :, :], AX_X, ALU.add))
                own_c.link(dve.reciprocal(g2[:, :], g1[:, :]))
                own_c.step(dve.tensor_tensor(PR[:, :, :], EX[:, :, :], bc(g2[:, :]), ALU.mult))
                own_c.wait()
                apart(dve)
                for c in range(NT):
                    last = dve.max(M8[:, c, :], PR[:, c, :])
                own_c.step(last)
                own_c.wait()
                apart(dve)
                for c in range(NT):
                    last = dve.max_index(I8[:, c, :], M8[:, c, :], PR[:, c, :])
                own_c.link(last)
                own_c.link(dve.tensor_copy(IF[:, :, :], I8[:, :, 0:2]))
                experts = iota[:, :].unsqueeze(1).to_broadcast([P, NT, E])
                dve.tensor_tensor(K0[:, :, :], experts, bc(IF[:, :, 0]), ALU.is_equal)
                own_c.link(dve.tensor_tensor(K1[:, :, :], experts, bc(IF[:, :, 1]), ALU.is_equal))
                own_c.link(dve.tensor_tensor(K0[:, :, :], K0[:, :, :], K1[:, :, :], ALU.add))
                own_c.link(dve.tensor_tensor(K1[:, :, :], PR[:, :, :], K0[:, :, :], ALU.mult))
                own_c.link(dve.tensor_reduce(g1[:, :], K1[:, :, :], AX_X, ALU.add))
                own_c.link(dve.reciprocal(g2[:, :], g1[:, :]))
                dve.tensor_tensor(WT[:, :, :], K1[:, :, :], bc(g2[:, :]), ALU.mult).then_inc(wt_ready.sem, 1)

            def c_bias(b):
                dve.wait_ge(y_full.sem, y_full.at(b, NY))
                dve.wait_ge(y_taken.sem, y_taken.at(b, NY - 1))
                dve.tensor_tensor(RES[:, :, :], tokens(psY[:, :]), RES[:, :, :], ALU.add).then_inc(y_taken.sem, 1)

            def add_expert(b, e):
                dve.wait_ge(y_full.sem, y_full.at(b, 3 + e))
                dve.wait_ge(y_taken.sem, y_taken.at(b, 2 + e))
                if e == 0:
                    dve.wait_ge(wt_ready.sem, wt_ready.at(b, 1))
                for c in range(NT):
                    last = dve.scalar_tensor_tensor(out=RES[:, c, :], in0=chunk(psY, c), scalar=WT[:, c, e:e + 1],
                                                    in1=RES[:, c, :], op0=ALU.mult, op1=ALU.add)
                last.then_inc(y_taken.sem, 1)
                if e == E - 1:
                    own_c.end()

            HEAD = {20: (head_stats,), 22: (head_norm,), 25: (head_mixes,), 28: (wkv_args,)}
            TAIL = {4: (wkv_scans,), 5: (wkv_out,), 8: (stats_1,), 9: (norm_1,), 12: (mixes,), 17: (stats_2,), 19: (norm_2,),
                    22: (split_qk,), 23: (take_qt(0),), 25: (take_qt(1),), 27: (take_qt(2),), 28: (take_qt(3),)}
            POST = {2: (c_ctx,), 3: (c_norm,), 5: (c_gate,), 9: (c_top,)}

            def turn(tail, head, core, post, slots=range(SLOTS)):
                for s in slots:
                    g, k = divmod(s, PER)
                    nxt = core if g + 1 < NG else tail
                    extras(s, (post, POST), (tail, TAIL), (head, HEAD))
                    if k < NT and nxt is not None:
                        maxima(nxt, (g + 1) % NG, k)
                    if k == 4 and core is not None:
                        context_t(core, g)
                    if k == 6 and core is not None:
                        context(core, g)
                    if post is not None and k in (3, 6):
                        e = 2 * g - (1 if k == 6 else 2)
                        if e >= 0:
                            add_expert(post, e)
                if post is not None:
                    add_expert(post, E - 2)
                    add_expert(post, E - 1)
                    c_bias(post)
                if isinstance(tail, int) and tail == 0:
                    split_w1()

            over(dve, turn)


_INS = VEC + SQUARE + ["L0_attn_x", "L0_attn_Wck", "L0_attn_Wcv", "L0_ffn_Wg", "L0_ffn_W1", "L0_ffn_b1",
                       "L0_ffn_W2", "L0_ffn_b2"]


def kernel(**inputs):
    import numpy as _np
    import concourse.bacc as _bacc
    from concourse import mybir as _mybir
    from concourse.bass_utils import run_bass_kernel_spmd as _run

    nc = _bacc.Bacc("TRN2", target_bir_lowering=False, num_devices=1)
    arrays, args = {}, {}
    for name in _INS:
        a = _np.ascontiguousarray(inputs[name])
        arrays[f"in_{name}_dram"] = a
        args[name] = nc.dram_tensor(f"in_{name}_dram", a.shape, _mybir.dt.from_np(a.dtype), kind="ExternalInput").ap()
    shape = inputs["L0_attn_x"].shape
    out = nc.dram_tensor("out_0_dram", shape, _mybir.dt.float32, kind="ExternalOutput").ap()
    build(nc, args, out)
    r = _run(nc, [arrays], core_ids=[0])
    return r.results[0]["out_0_dram"]
```

```python
from contextlib import ExitStack

import concourse.bass as bass
from concourse import mybir

F32 = mybir.dt.float32
F32R = mybir.dt.float32r
U32 = mybir.dt.uint32
ALU = mybir.AluOpType
ACT = mybir.ActivationFunctionType
AX_X = mybir.AxisListType.X

P = 128
EPS = 1e-5
VEC = ["L0_attn_ln0_g", "L0_attn_ln0_b", "L0_attn_ln1_g", "L0_attn_ln1_b", "L0_attn_time_decay",
       "L0_attn_time_first", "L0_attn_tm_k", "L0_attn_tm_v", "L0_attn_tm_r", "L0_attn_cm_k",
       "L0_attn_cm_r", "L0_ffn_ln1_g", "L0_ffn_ln1_b", "L0_ffn_ln2_g", "L0_ffn_ln2_b"]
SQUARE = ["L0_attn_Wk", "L0_attn_Wv", "L0_attn_Wr", "L0_attn_Wo", "L0_attn_Wcr",
          "L0_ffn_Wq", "L0_ffn_Wk", "L0_ffn_Wv", "L0_ffn_Wo"]


class Signal:

    def __init__(self, handle, per, start):
        self.sem, self.per, self.start = handle, per, start

    def at(self, b, k):
        return b * self.per + (k + self.start)

    def due(self, b, k):
        return not isinstance(b, int) or self.at(b, k) > self.start


class Chain:

    def __init__(self, engine, handle, per):
        self.engine, self.sem, self.per = engine, handle, per

    def begin(self, b, k=0):
        self.b, self.k = b, k

    def step(self, instruction):
        self.k += 1
        instruction.then_inc(self.sem, 1)

    def wait(self):
        self.engine.wait_ge(self.sem, self.b * self.per + self.k)

    def link(self, instruction):
        self.step(instruction)
        self.wait()

    def end(self):
        assert self.k == self.per, (self.sem, self.k, self.per)


def build(nc, t, out):
    x = t["L0_attn_x"]
    B, T, C = x.shape
    NT = T // P
    F = t["L0_attn_Wck"].shape[1]
    NF = F // P
    E = t["L0_ffn_Wg"].shape[1]
    H, DH = 16, C // 16
    G = 4
    NG = H // G
    HW = P // G
    RS = 3 * DH
    RM = RS + 2
    SCALE = float(DH) ** -0.5
    NEG = -1e38
    assert C == P and T == 512 and E == 8 and NF == 4

    with ExitStack() as ctx:
        def sb(name, shape, dt=F32):
            return ctx.enter_context(nc.sbuf_tensor(name, shape, dt))

        def bank(name, shape):
            return ctx.enter_context(nc.psum_tensor(name, shape, F32))

        def sig(name, per=1, start=0):
            return Signal(ctx.enter_context(nc.semaphore(name)), per, start)

        def sem(name):
            return ctx.enter_context(nc.semaphore(name))

        sq = {n: sb(n, [P, C]) for n in SQUARE}
        wck = sb("wck", [P, F])
        wcv = sb("wcv", [P, NF, C])
        wg = sb("wg", [P, E])
        b2 = sb("b2", [E, C])
        w1h = sb("w1h", [P, E, F], F32R)
        w1l = sb("w1l", [P, E, F], F32R)
        w2 = sb("w2", [P, E, NF, C])
        NV = len(VEC)
        rows = sb("rows", [NV + E * NF, P])
        cols = sb("cols", [P, NV + E * NF])
        ident = sb("ident", [P, P])
        half = sb("half", [P, NT])
        iota = sb("iota", [P, E])
        idle = sb("idle", [P, 2, 16])
        idle_turn = [0, 0]
        idle_act = sb("idle_act", [P, 1])
        idle_dve = sb("idle_dve", [P, 1])
        wdec = sb("wdec", [P, 1])
        wrow = sb("wrow", [P, T])
        col = {n: cols[:, i:i + 1] for i, n in enumerate(VEC)}

        X = sb("X", [P, NT, C])
        Z0 = sb("Z0", [P, NT, C])
        ZA = sb("ZA", [P, NT, C])
        XA = sb("XA", [P, T + 1])
        D = sb("D", [P, T])
        MK = sb("MK", [P, T])
        MV = sb("MV", [P, T])
        MR = sb("MR", [P, T])
        K = sb("K", [P, T])
        V = sb("V", [P, T])
        R = sb("R", [P, T])
        PP = sb("PP", [P, T + 1])
        EE = sb("EE", [P, 4, T])
        EV = sb("EV", [P, T])
        AA = sb("AA", [P, T + 1])
        BB = sb("BB", [P, T + 1])
        N2 = K
        D1 = D
        DD = EV
        N1 = EV
        GT = MV
        Y1 = sb("Y1", [P, NT, C])
        KK = EE
        RT = Z0
        X1 = sb("X1", [P, NT, C])
        Z1 = sb("Z1", [P, NT, C])
        HT = sb("HT", [P, T])
        QA = sb("QA", [P, NT, H, HW])
        KA = sb("KA", [P, NT, H, HW])
        VA = sb("VA", [P, NT, H, HW])
        KT = sb("KT", [P, NG, T], F32R)
        Q1 = sb("Q1", [P, NG, T], F32R)
        stA = sb("stA", [P, NT, 6])
        mvA = sb("mvA", [P, NT, 2])
        rsA = sb("rsA", [P, 4, NT])
        stH = sb("stH", [P, NT, 6])
        mvH = sb("mvH", [P, NT, 2])
        rsH = sb("rsH", [P, 4, NT])

        NM = sb("NM", [P, NT, H])
        Q2 = sb("Q2", [P, 2, T], F32R)
        PT = sb("PT", [P, 2 * G, T])
        CT = sb("CT", [P, T])
        RD = sb("RD", [P, NT, G])
        CX = sb("CX", [P, NT, H, DH])
        Z1b = sb("Z1b", [P, NT, C])

        CXT = sb("CXT", [P, T])
        Y3 = sb("Y3", [P, NT, C])
        XZ = sb("XZ", [P, NT, C])
        RES = sb("RES", [P, NT, C])
        ZM = sb("ZM", [P, NT, C])
        MT = sb("MT", [P, T])
        MH = sb("MH", [P, T], F32R)
        ML = sb("ML", [P, T], F32R)
        H1 = sb("H1", [P, 2, NF, T])
        w1 = H1[:, :, :, :].rearrange("p a f t -> p (a f t)").rearrange("p (e f) -> p e f", e=E)
        stC = sb("stC", [P, NT, 6])
        mvC = sb("mvC", [P, NT, 2])
        rsC = sb("rsC", [P, 4, NT])
        EX = sb("EX", [P, NT, E])
        PR = sb("PR", [P, NT, E])
        M8 = sb("M8", [P, NT, 8])
        I8 = sb("I8", [P, NT, 8], U32)
        IF = sb("IF", [P, NT, 2])
        K0 = sb("K0", [P, NT, E])
        K1 = sb("K1", [P, NT, E])
        g1 = sb("g1", [P, NT])
        g2 = sb("g2", [P, NT])
        WT = sb("WT", [P, NT, E])
        WTT = CXT[0:E, :]

        psA = bank("psA", [P, 2, T])
        psS = bank("psS", [P, 2, T])
        psT = bank("psT", [P, 2, T])
        psV = bank("psV", [P, T])
        psY = bank("psY", [P, T])

        s_vec = sem("s_vec")
        s_sq = sem("s_sq")
        s_w1 = sem("s_w1")
        s_w2 = sem("s_w2")
        s_ident = sem("s_ident")
        s_const = sem("s_const")
        s_colT = sem("s_colT")
        s_cols = sem("s_cols")
        s_dec = sem("s_dec")
        s_wrow = sem("s_wrow")
        s_w1s = sem("s_w1s")

        USES = ["out", "kt2", "qt2", "rows", "kt3", "logits", "qt3", "q2_1", "wo", "xc", "gate", "kk0",
                "kk1", "bias", "q2_2", "kk2", "kk3", "rr", "kv", "zh", "k", "kt0", "q2_3", "q",
                "ZA", "qt0", "K", "V", "R", "kt1", "qt1", "q2_0", "v", "ctx"]
        assert len(USES) % 2 == 0
        a_full = sem("a_full_0"), sem("a_full_1")
        a_taken = sem("a_taken_0"), sem("a_taken_1")

        def turns_late(u):
            if u in ("out", "rows", "logits", "gate", "bias"):
                return 2
            return -1 if u.isupper() else int(u in ("q2_1", "q2_2", "q2_3", "kt2", "qt2", "kt3", "qt3", "ctx"))

        def uses_before(b, name):
            late, at = turns_late(name), USES.index(name)
            return sum(0 <= n - turns_late(u) < B and (n < b + late or i < at)
                       for n in range(-1, b + late + 1) for i, u in enumerate(USES))

        class use:

            def __init__(self, b, name):
                self.b = 0 if isinstance(b, int) else b
                uses = uses_before(b, name) if isinstance(b, int) else uses_before(4, name) - 4 * len(USES)
                self.bank, self.full, self.taken = psA[:, uses % 2, :], a_full[uses % 2], a_taken[uses % 2]
                self.uses = uses // 2

            @property
            def before(self):
                return self.b * (len(USES) // 2) + self.uses

            @property
            def after(self):
                return self.b * (len(USES) // 2) + (self.uses + 1)

        x_in = sig("x_in", 16)
        x_used = sig("x_used")
        h_stats = sig("h_stats")
        h_rstd = sig("h_rstd")
        zh_ready = sig("zh_ready")
        hd_ready = sig("hd_ready")
        hmix_ready = sig("hmix_ready", 3)
        a_stats = sig("a_stats", 2)
        a_rstd = sig("a_rstd", 2)
        za_ready = sig("za_ready", 2)
        d_ready = sig("d_ready")
        mix_ready = sig("mix_ready", 2)
        args_ready = sig("args_ready")
        exps_ready = sig("exps_ready")
        r_ready = sig("r_ready")
        n2_ready = sig("n2_ready")
        bb_ready = sig("bb_ready")
        d1_ready = sig("d1_ready")
        g_ready = sig("g_ready")
        kk_ready = sig("kk_ready", NF)
        y1x_ready = sig("y1x_ready")
        rt_ready = sig("rt_ready")
        z1_ready = sig("z1_ready")
        hi_ready = sig("hi_ready", 2)
        hi_copied = sig("hi_copied", 2)

        NS = NG * NT * G
        s_full = sig("s_full", NS)
        s_taken = sig("s_taken", NS)
        t_full = sig("t_full", NS)
        t_taken = sig("t_taken", NS)
        m_ready = sig("m_ready", NG)
        v_full = sig("v_full", NG * NT)
        c_full = sig("c_full", NG)
        ct_ready = sig("ct_ready", NG)
        cx_ready = sig("cx_ready", NG)
        kept = sig("kept")

        h_full = sig("h_full", E * NF)
        h_taken = sig("h_taken", E * NF, start=1)
        y_full = sig("y_full", E, start=1)
        y_taken = sig("y_taken", E, start=1)

        SCORES, SCORES_0 = (0, 4, 4, 4, 4, 0, 0, 0), (0, 4, 4, 4, 4, 0, 0, 0)

        def score_tiles(g, k):
            a = SCORES if g else SCORES_0
            return range(sum(a[:k]), sum(a[:k + 1]))

        def expert_chunk(s):
            return divmod((s - 6) % SLOTS, NT)

        c_stats = sig("c_stats")
        c_rstd = sig("c_rstd")
        zm_ready = sig("zm_ready")
        ml_ready = sig("ml_ready")
        ex_ready = sig("ex_ready")
        wt_ready = sig("wt_ready")
        out_done = sig("out_done", 16, start=16)

        dve_h, dve_a, dve_c = sem("dve_h"), sem("dve_a"), sem("dve_c")
        dve_m, dve_x = sem("dve_m"), sem("dve_x")
        pool_h, pool_a, pool_c = sem("pool_h"), sem("pool_a"), sem("pool_c")

        def chunk(ap, c):
            return ap[:, c * P:(c + 1) * P]

        def heads(ap):
            return ap.rearrange("p (c h d) -> p c h d", h=H, d=DH)

        def tokens(ap):
            return ap.rearrange("p (c n) -> p c n", c=NT)

        def apart(engine):
            i = int(engine is nc.gpsimd)
            idle_turn[i] = (idle_turn[i] + 1) % 16
            unread = idle[:, i, idle_turn[i]:idle_turn[i] + 1]
            if engine is nc.gpsimd:
                engine.tensor_tensor(unread, half[:, 0:1], half[:, 0:1], ALU.mult)
            else:
                engine.tensor_copy(unread, half[:, 0:1])

        SLOTS, PER = 8 * NG, 8
        FIRST, FIRST_HEAD = 6, 20

        def roles(tail, head, core, post, first=FIRST):
            for s in range(first, SLOTS):
                yield s, tail, head, core, post, None
            for s in range(FIRST):
                yield s, head, None, tail, core, post

        def over(engine, turn):
            turn(None, 0, None, None, FIRST_HEAD)
            turn(0, 1, None, None)
            turn(1, 2, 0, None)
            turn(2, 3, 1, 0)
            with engine.Fori(3, B - 1) as n:
                turn(n, n + 1, n - 1, n - 2)
            turn(B - 1, None, B - 2, B - 3)
            turn(None, None, B - 1, B - 2)
            turn(None, None, None, B - 1)

        def extras(s, *parts):
            for b, table in parts:
                if b is not None:
                    for step in table.get(s, ()):
                        step(b)

        block = ctx.enter_context(nc.Block())

        @block.sync
        def _(sp):
            def load(b):
                if x_used.due(b, 0):
                    sp.wait_ge(x_used.sem, x_used.at(b, 0))
                sp.dma_start(X[:, :, :], x[b].rearrange("(c p) n -> p c n", p=P)).then_inc(x_in.sem, 16)

            load(0)
            for i, n in enumerate(VEC):
                sp.dma_start(rows[i:i + 1, :], t[n].rearrange("(a n) -> a n", a=1)).then_inc(s_vec, 16)
            sp.dma_start(rows[NV:NV + E * NF, :],
                         t["L0_ffn_b1"].rearrange("e (c p) -> (e c) p", p=P)).then_inc(s_vec, 16)

            def store(b):
                sp.wait_ge(y_taken.sem, y_taken.at(b, E))
                sp.dma_start(out[b].rearrange("(c p) n -> p c n", p=P), RES[:, :, :]).then_inc(out_done.sem, 16)

            sp.sem_inc(out_done.sem, 16)
            sp.sem_inc(y_full.sem, 1)
            for n in SQUARE:
                sp.dma_start(sq[n][:, :], t[n]).then_inc(s_sq, 16)
            sp.dma_start(wck[:, :], t["L0_attn_Wck"]).then_inc(s_sq, 16)
            sp.dma_start(wcv[:, :, :], t["L0_attn_Wcv"].rearrange("(c p) n -> p c n", p=P)).then_inc(s_sq, 16)
            sp.dma_start(wg[:, :], t["L0_ffn_Wg"]).then_inc(s_sq, 16)
            sp.dma_start(b2[:, :], t["L0_ffn_b2"]).then_inc(s_sq, 16)
            sp.dma_start(w1, t["L0_ffn_W1"].rearrange("e p f -> p e f")).then_inc(s_w1, 16)
            sp.dma_start(w2[:, :, :, :], t["L0_ffn_W2"].rearrange("e (c p) n -> p e c n", p=P)).then_inc(s_w2, 16)
            load(1)
            load(2)
            with sp.Fori(2, B - 1) as n:
                load(n + 1)
                store(n - 2)
            for b in range(B - 3, B):
                store(b)
            sp.wait_ge(out_done.sem, out_done.at(B - 1, 16))

        N_VEC, N_SQ, N_CONST = 16 * (NV + 1), 16 * (len(SQUARE) + 4), 10 + E

        @block.gpsimd
        def _(pool):
            pool.memset(ident[:, :], 0.0).then_inc(s_ident, 1)
            pool.wait_ge(s_ident, 1)
            pool.affine_select(out=ident[:, :], in_=ident[:, :], compare_op=ALU.not_equal, fill=1.0, base=0,
                               pattern=[[-1, P]], channel_multiplier=1).then_inc(s_ident, 1)
            pool.memset(half[:, :], -0.5).then_inc(s_const, 1)
            for e in range(E):
                pool.memset(iota[:, e:e + 1], float(e)).then_inc(s_const, 1)
            pool.memset(XA[:, 0:1], 0.0).then_inc(s_const, 1)
            pool.memset(PP[:, 0:1], NEG).then_inc(s_const, 1)
            pool.memset(AA[:, 0:1], 0.0).then_inc(s_const, 1)
            pool.memset(BB[:, 0:1], 0.0).then_inc(s_const, 1)
            pool.memset(QA[:, :, :, RS:HW], 0.0).then_inc(s_const, 1)
            pool.memset(KA[:, :, :, RM:HW], 0.0).then_inc(s_const, 1)
            pool.memset(KA[:, :, :, RS:RM], 1.0).then_inc(s_const, 1)
            pool.memset(VA[:, :, :, DH + 1:HW], 0.0).then_inc(s_const, 1)
            pool.memset(VA[:, :, :, DH:DH + 1], 1.0).then_inc(s_const, 1)
            pool.wait_ge(s_const, N_CONST)

            own_h = Chain(pool, pool_h, 6)
            own_a = Chain(pool, pool_a, 8)
            own_c = Chain(pool, pool_c, 1)

            def rstd(own, mv, rs, both):
                var = mv[:, :, 1]
                own.link(pool.tensor_scalar(rs[:, 1, :], var, EPS, None, ALU.add))
                last = pool.tensor_tensor(rs[:, 0, :], rs[:, 1, :], half[:, :], ALU.pow)
                if not both:
                    return last
                own.link(last)
                own.link(pool.tensor_tensor(rs[:, 1, :], rs[:, 0, :], rs[:, 0, :], ALU.mult))
                own.step(pool.tensor_tensor(rs[:, 1, :], rs[:, 1, :], var, ALU.mult))
                own.wait()
                apart(pool)
                own.link(pool.tensor_scalar(rs[:, 1, :], rs[:, 1, :], EPS, None, ALU.add))
                own.link(pool.tensor_tensor(rs[:, 2, :], rs[:, 1, :], half[:, :], ALU.pow))
                return pool.tensor_tensor(rs[:, 3, :], rs[:, 2, :], rs[:, 0, :], ALU.mult)

            def shift(b, u):
                pool.wait_ge(use(b, u).taken, use(b, u).after)
                return pool.tensor_tensor(D[:, :], XA[:, 1:T + 1], XA[:, 0:T], ALU.subtract)

            def head_norm(b):
                own_h.begin(b)
                pool.wait_ge(h_stats.sem, h_stats.at(b, 1))
                apart(pool)
                rstd(own_h, mvH, rsH, True).then_inc(h_rstd.sem, 1)
                own_h.end()

            def head_shift(b):
                shift(b, "ZA").then_inc(hd_ready.sem, 1)

            def head_sigmoid(b):
                pool.wait_ge(use(b, "R").taken, use(b, "R").after)
                apart(pool)
                pool.tensor_scalar(R[:, :], R[:, :], 0.5, 0.5, ALU.mult, ALU.add).then_inc(r_ready.sem, 1)

            def side(b):
                pool.wait_ge(exps_ready.sem, exps_ready.at(b, 1))
                pool.tensor_tensor(N2[:, :], EE[:, 3, :], V[:, :], ALU.mult).then_inc(n2_ready.sem, 1)

            def wkv_out(b):
                own_a.begin(b)
                pool.wait_ge(bb_ready.sem, bb_ready.at(b, 1))
                own_a.link(pool.tensor_tensor(D1[:, :], EE[:, 2, :], BB[:, 0:T], ALU.mult))
                pool.tensor_tensor(D1[:, :], D1[:, :], EE[:, 3, :], ALU.add).then_inc(d1_ready.sem, 1)

            def residual(b):
                pool.wait_ge(za_ready.sem, za_ready.at(b, 1))
                pool.tensor_tensor(Y1[:, :, :], Y1[:, :, :], X[:, :, :], ALU.add).then_inc(y1x_ready.sem, 1)

            def sigmoid(b):
                pool.wait_ge(use(b, "rr").taken, use(b, "rr").after)
                apart(pool)
                pool.tensor_scalar(RT[:, :, :], RT[:, :, :], 0.5, 0.5, ALU.mult, ALU.add).then_inc(rt_ready.sem, 1)

            def norm_1(b):
                own_a.begin(b, 1)
                pool.wait_ge(a_stats.sem, a_stats.at(b, 1))
                apart(pool)
                rstd(own_a, mvA, rsA, False).then_inc(a_rstd.sem, 1)

            def tail_shift(b):
                shift(b, "xc").then_inc(d_ready.sem, 1)

            def square(b):
                for f in range(NF):
                    pool.wait_ge(use(b, f"kk{f}").taken, use(b, f"kk{f}").after)
                    pool.tensor_tensor(KK[:, f, :], KK[:, f, :], KK[:, f, :], ALU.mult).then_inc(kk_ready.sem, 1)

            def norm_2(b):
                own_a.begin(b, 2)
                pool.wait_ge(a_stats.sem, a_stats.at(b, 2))
                apart(pool)
                rstd(own_a, mvA, rsA, True).then_inc(a_rstd.sem, 1)
                own_a.end()

            def residual_2(b):
                pool.wait_ge(a_rstd.sem, a_rstd.at(b, 2))
                apart(pool)
                for c in range(NT):
                    last = pool.tensor_scalar(Z1[:, c, :], X1[:, c, :], mvA[:, c, 0:1], rsA[:, 0, c:c + 1],
                                              ALU.subtract, ALU.mult)
                last.then_inc(z1_ready.sem, 1)

            def keep(b):
                pool.wait_ge(z1_ready.sem, z1_ready.at(b, 1))
                if y_taken.due(b - 1, 1):
                    pool.wait_ge(y_taken.sem, y_taken.at(b - 1, 1))
                pool.tensor_tensor(XZ[:, :, :], X1[:, :, :], Z1[:, :, :], ALU.add)
                pool.tensor_scalar(Z1b[:, :, :], Z1[:, :, :], 1.0, None, ALU.mult).then_inc(kept.sem, 1)

            def c_norm(b):
                own_c.begin(b)
                pool.wait_ge(c_stats.sem, c_stats.at(b, 1))
                apart(pool)
                rstd(own_c, mvC, rsC, False).then_inc(c_rstd.sem, 1)
                own_c.end()

            def c_split(b):
                pool.wait_ge(use(b, "rows").taken, use(b, "rows").after)
                pool.tensor_tensor(ML[:, :], MT[:, :], MH[:, :].bitcast(F32), ALU.subtract).then_inc(ml_ready.sem, 1)

            HEAD = {20.5: (head_norm,), 23: (head_shift,), 26.5: (head_sigmoid,)}
            TAIL = {1: (side,), 3.5: (wkv_out,), 9: (norm_1,), 10.5: (tail_shift,), 11.5: (residual,),
                    13: (square,), 15.5: (sigmoid,), 16.5: (norm_2,), 18: (residual_2,)}
            CORE = {12: (keep,)}
            POST = {0: (c_norm,), 3: (c_split,)}

            def turn(*elements):
                for s, tail, head, core, post, past in roles(*elements):
                    for at in (s, s + 0.5):
                        extras(at, (post, POST), (core, CORE), (tail, TAIL), (head, HEAD))

            over(pool, turn)

        @block.scalar
        def _(act):
            act.wait_ge(s_colT, 1)
            act.activation(cols[:, :], psA[:, 0, 0:NV + E * NF], ACT.Copy).then_inc(s_cols, 1)
            act.wait_ge(s_cols, 1)
            act.activation(wdec[:, :], col["L0_attn_time_decay"], ACT.Exp).then_inc(s_dec, 1)
            act.wait_ge(s_const, N_CONST)
            act.activation(idle_act[:, :], half[:, 0:1], ACT.Copy).then_inc(h_taken.sem, 1)

            def affine(dst, src, g, c):
                return act.activation(dst, src, ACT.Identity, bias=col[c], scale=col[g])

            def head_rows(b):
                act.wait_ge(use(b, "ZA").full, use(b, "ZA").after)
                affine(XA[:, 1:T + 1], use(b, "ZA").bank, "L0_attn_ln0_g", "L0_attn_ln0_b").then_inc(use(b, "ZA").taken, 1)

            def head_k(b):
                act.wait_ge(use(b, "K").full, use(b, "K").after)
                act.activation(K[:, :], use(b, "K").bank, ACT.Copy).then_inc(use(b, "K").taken, 1)

            def head_v(b):
                act.wait_ge(use(b, "V").full, use(b, "V").after)
                act.activation(V[:, :], use(b, "V").bank, ACT.Copy).then_inc(use(b, "V").taken, 1)

            def head_r(b):
                act.wait_ge(use(b, "R").full, use(b, "R").after)
                act.activation(R[:, :], use(b, "R").bank, ACT.Tanh, scale=0.5).then_inc(use(b, "R").taken, 1)

            def wkv_exps(b):
                act.wait_ge(args_ready.sem, args_ready.at(b, 1))
                act.activation(EE[:, :, :], EE[:, :, :], ACT.Exp).then_inc(exps_ready.sem, 1)

            def rows_1(b):
                act.wait_ge(use(b, "xc").full, use(b, "xc").after)
                affine(XA[:, 1:T + 1], use(b, "xc").bank, "L0_attn_ln1_g", "L0_attn_ln1_b").then_inc(use(b, "xc").taken, 1)

            def relu(f):
                def step(b):
                    act.wait_ge(use(b, f"kk{f}").full, use(b, f"kk{f}").after)
                    act.activation(KK[:, f, :], use(b, f"kk{f}").bank, ACT.Relu).then_inc(use(b, f"kk{f}").taken, 1)
                return step

            def receptance(b):
                act.wait_ge(use(b, "rr").full, use(b, "rr").after)
                act.activation(RT[:, :, :], tokens(use(b, "rr").bank), ACT.Tanh, scale=0.5).then_inc(use(b, "rr").taken, 1)

            def rows_2(b):
                act.wait_ge(use(b, "zh").full, use(b, "zh").after)
                affine(HT[:, :], use(b, "zh").bank, "L0_ffn_ln1_g", "L0_ffn_ln1_b").then_inc(use(b, "zh").taken, 1)

            def split_k(b):
                act.wait_ge(use(b, "k").full, use(b, "k").after)
                act.activation(KA[:, :, :, 0:DH].bitcast(F32R), heads(use(b, "k").bank), ACT.Copy).then_inc(hi_ready.sem, 1)
                act.wait_ge(hi_ready.sem, hi_ready.at(b, 1))
                act.activation(KA[:, :, :, 2 * DH:RS], KA[:, :, :, 0:DH], ACT.Copy).then_inc(hi_copied.sem, 1)

            def split_q(b):
                act.wait_ge(use(b, "q").full, use(b, "q").after)
                act.activation(QA[:, :, :, 0:DH].bitcast(F32R), heads(use(b, "q").bank), ACT.Copy).then_inc(hi_ready.sem, 1)
                act.wait_ge(hi_ready.sem, hi_ready.at(b, 2))
                act.activation(QA[:, :, :, DH:2 * DH], QA[:, :, :, 0:DH], ACT.Copy).then_inc(hi_copied.sem, 1)

            def take_kt(g):
                def step(b):
                    act.wait_ge(use(b, f"kt{g}").full, use(b, f"kt{g}").after)
                    act.activation(KT[:, g, :], use(b, f"kt{g}").bank, ACT.Copy).then_inc(use(b, f"kt{g}").taken, 1)
                return step

            def take_qt(g):
                def step(b):
                    act.wait_ge(use(b, f"qt{g}").full, use(b, f"qt{g}").after)
                    act.activation(Q1[:, g, :], use(b, f"qt{g}").bank, ACT.Copy).then_inc(use(b, f"qt{g}").taken, 1)
                return step

            def take_v(b):
                if v_full.due(b, 0):
                    act.wait_ge(v_full.sem, v_full.at(b, 0))
                act.wait_ge(use(b, "v").full, use(b, "v").after)
                act.activation(VA[:, :, :, 0:DH], heads(use(b, "v").bank), ACT.Copy).then_inc(use(b, "v").taken, 1)

            def q2(b, g):
                act.wait_ge(use(b, f"q2_{g}").full, use(b, f"q2_{g}").after)
                act.activation(Q2[:, g % 2, :], use(b, f"q2_{g}").bank, ACT.Copy).then_inc(use(b, f"q2_{g}").taken, 1)

            def exps(b, g, c, j):
                n = g * NT * G + c * G + j
                if j == 0 and v_full.due(b, g * NT + c - 1):
                    act.wait_ge(v_full.sem, v_full.at(b, g * NT + c - 1))
                act.wait_ge(t_full.sem, t_full.at(b, n + 1))
                act.activation(PT[:, (c % 2) * G + j, :], psT[:, n % 2, :], ACT.Exp,
                               scale=SCALE).then_inc(t_taken.sem, 1)

            def c_ctx(b):
                act.wait_ge(use(b, "ctx").full, use(b, "ctx").after)
                act.activation(CXT[:, :], use(b, "ctx").bank, ACT.Copy).then_inc(use(b, "ctx").taken, 1)

            def c_norm(b):
                act.wait_ge(use(b, "rows").full, use(b, "rows").after)
                affine(MH[:, :], use(b, "rows").bank, "L0_ffn_ln2_g", "L0_ffn_ln2_b")
                affine(MT[:, :], use(b, "rows").bank, "L0_ffn_ln2_g", "L0_ffn_ln2_b").then_inc(use(b, "rows").taken, 1)

            def c_gate(b):
                act.wait_ge(use(b, "logits").taken, use(b, "logits").after)
                act.activation(EX[:, :, :], EX[:, :, :], ACT.Exp).then_inc(ex_ready.sem, 1)

            def c_gate_t(b):
                act.wait_ge(use(b, "gate").full, use(b, "gate").after)
                act.activation(WTT, use(b, "gate").bank[0:E, :], ACT.Copy).then_inc(use(b, "gate").taken, 1)

            def gelu(b, e, f):
                if f == 0 and y_full.due(b, e - 1):
                    act.wait_ge(y_full.sem, y_full.at(b, e - 1))
                act.wait_ge(h_full.sem, h_full.at(b, e * NF + f + 1))
                act.activation(H1[:, e % 2, f, :], psT[:, f % 2, :], ACT.Gelu_apprx_tanh,
                               bias=cols[:, NV + e * NF + f:NV + e * NF + f + 1]).then_inc(h_taken.sem, 1)

            HEAD = {22.5: (head_rows,), 25: (head_k,), 25.5: (head_v,), 26: (head_r,)}
            TAIL = {0: (wkv_exps,), 10: (rows_1,), 12: (relu(0),), 12.5: (relu(1),), 14: (relu(2),),
                    15: (relu(3), receptance,), 19: (rows_2,), 20: (split_k,), 21: (take_kt(0),), 22: (split_q,),
                    23.5: (take_qt(0),), 27: (take_kt(1),), 27.5: (take_qt(1),), 29.5: (take_v,)}
            CORE = {0.5: (take_kt(2),), 1: (take_qt(2),), 2: (take_kt(3),), 3: (take_qt(3),)}
            POST = {2: (c_norm,), 4: (c_gate,), 11: (c_gate_t,)}

            def turn(*elements):
                for s, tail, head, core, post, past in roles(*elements):
                    g, k = divmod(s, PER)
                    for i in range(2):
                        extras(s + i / 2, (post, POST), (core, CORE), (head, HEAD), (tail, TAIL))
                        if k < NT and core is not None:
                            exps(core, g, k, 2 * i)
                            exps(core, g, k, 2 * i + 1)
                        if k >= NT and post is not None:
                            gelu(post, 2 * g + (k - NT) // 2, (k - NT) % 2 * 2 + i)
                        if k == 5 and i == 0:
                            nxt = core if g + 1 < NG else tail
                            if nxt is not None:
                                q2(nxt, (g + 1) % NG)
                    if s == SLOTS - 1 and core is not None:
                        c_ctx(core)

            over(act, turn)

        @block.tensor
        def _(pe):
            pe.wait_ge(s_ident, 2)
            pe.wait_ge(s_vec, N_VEC)
            pe.transpose(psA[:, 0, 0:NV + E * NF], rows[:, :], ident[0:NV + E * NF, 0:NV + E * NF]).then_inc(s_colT, 1)
            pe.wait_ge(s_cols, 1)
            pe.wait_ge(s_const, N_CONST)
            pe.wait_ge(s_sq, N_SQ)

            def transposes(dst, src):
                for c in range(NT):
                    last = pe.transpose(chunk(dst, c), src[:, c, :], ident[:, :])
                return last

            def to_tokens(dst, src, w):
                for c in range(NT):
                    last = pe.matmul(chunk(dst, c), chunk(src, c), w, start=True, stop=True)
                return last

            def head_rows(b):
                pe.wait_ge(zh_ready.sem, zh_ready.at(b, 1))
                if not isinstance(b, int) or b > 0:
                    pe.wait_ge(use(b, "ZA").taken, use(b, "ZA").before)
                transposes(use(b, "ZA").bank, ZA).then_inc(use(b, "ZA").full, 1)

            def head_k(b):
                pe.wait_ge(hmix_ready.sem, hmix_ready.at(b, 1))
                if not isinstance(b, int) or b > 0:
                    pe.wait_ge(use(b, "K").taken, use(b, "K").before)
                pe.matmul(use(b, "K").bank, sq["L0_attn_Wk"][:, :], MK[:, :], start=True, stop=True).then_inc(use(b, "K").full, 1)

            def head_v(b):
                pe.wait_ge(hmix_ready.sem, hmix_ready.at(b, 2))
                pe.wait_ge(use(b, "V").taken, use(b, "V").before)
                pe.matmul(use(b, "V").bank, sq["L0_attn_Wv"][:, :], MV[:, :], start=True, stop=True).then_inc(use(b, "V").full, 1)

            def head_r(b):
                pe.wait_ge(hmix_ready.sem, hmix_ready.at(b, 3))
                pe.wait_ge(use(b, "R").taken, use(b, "R").before)
                pe.matmul(use(b, "R").bank, sq["L0_attn_Wr"][:, :], MR[:, :], start=True, stop=True).then_inc(use(b, "R").full, 1)

            def time_mix_out(b):
                pe.wait_ge(g_ready.sem, g_ready.at(b, 1))
                pe.wait_ge(use(b, "wo").taken, use(b, "wo").before)
                to_tokens(use(b, "wo").bank, GT, sq["L0_attn_Wo"][:, :]).then_inc(use(b, "wo").full, 1)

            def rows_1(b):
                pe.wait_ge(za_ready.sem, za_ready.at(b, 1))
                pe.wait_ge(use(b, "xc").taken, use(b, "xc").before)
                transposes(use(b, "xc").bank, ZA).then_inc(use(b, "xc").full, 1)

            def channel_mix_in(f):
                def step(b):
                    if f == 0:
                        pe.wait_ge(mix_ready.sem, mix_ready.at(b, 1))
                    pe.wait_ge(use(b, f"kk{f}").taken, use(b, f"kk{f}").before)
                    pe.matmul(use(b, f"kk{f}").bank, chunk(wck, f), MK[:, :], start=True, stop=True).then_inc(use(b, f"kk{f}").full, 1)
                return step

            def receptance(b):
                pe.wait_ge(mix_ready.sem, mix_ready.at(b, 2))
                pe.wait_ge(use(b, "rr").taken, use(b, "rr").before)
                to_tokens(use(b, "rr").bank, MR, sq["L0_attn_Wcr"][:, :]).then_inc(use(b, "rr").full, 1)

            def channel_mix_out(dst):
                for c in range(NT):
                    for f in range(NF):
                        last = pe.matmul(chunk(dst, c), chunk(KK[:, f, :], c), wcv[:, f, :],
                                         start=(f == 0), stop=(f == NF - 1))
                return last

            def channel_mix(b):
                pe.wait_ge(kk_ready.sem, kk_ready.at(b, NF))
                pe.wait_ge(use(b, "kv").taken, use(b, "kv").before)
                channel_mix_out(use(b, "kv").bank).then_inc(use(b, "kv").full, 1)

            def rows_2(b):
                pe.wait_ge(za_ready.sem, za_ready.at(b, 2))
                pe.wait_ge(use(b, "zh").taken, use(b, "zh").before)
                transposes(use(b, "zh").bank, ZA).then_inc(use(b, "zh").full, 1)

            def project_k(b):
                pe.wait_ge(use(b, "zh").taken, use(b, "zh").after)
                pe.wait_ge(use(b, "k").taken, use(b, "k").before)
                to_tokens(use(b, "k").bank, HT, sq["L0_ffn_Wk"][:, :]).then_inc(use(b, "k").full, 1)

            def project_q(b):
                pe.wait_ge(use(b, "q").taken, use(b, "q").before)
                to_tokens(use(b, "q").bank, HT, sq["L0_ffn_Wq"][:, :]).then_inc(use(b, "q").full, 1)

            def project_v(b):
                pe.wait_ge(use(b, "v").taken, use(b, "v").before)
                to_tokens(use(b, "v").bank, HT, sq["L0_ffn_Wv"][:, :]).then_inc(use(b, "v").full, 1)

            def turn_k(g):
                def step(b):
                    pe.wait_ge(hi_copied.sem, hi_copied.at(b, 1))
                    pe.wait_ge(use(b, "k").taken, use(b, "k").after)
                    pe.wait_ge(use(b, f"kt{g}").taken, use(b, f"kt{g}").before)
                    transposes(use(b, f"kt{g}").bank, KA[:, :, g * G:(g + 1) * G, :].rearrange("p c h w -> p c (h w)")).then_inc(use(b, f"kt{g}").full, 1)
                return step

            def turn_q(g):
                def step(b):
                    pe.wait_ge(hi_copied.sem, hi_copied.at(b, 2))
                    pe.wait_ge(use(b, "q").taken, use(b, "q").after)
                    pe.wait_ge(use(b, f"qt{g}").taken, use(b, f"qt{g}").before)
                    transposes(use(b, f"qt{g}").bank, QA[:, :, g * G:(g + 1) * G, :].rearrange("p c h w -> p c (h w)")).then_inc(use(b, f"qt{g}").full, 1)
                return step

            def score(b, g, u):
                c, j = divmod(u, G)
                n = g * NT * G + u
                if u == 0:
                    pe.wait_ge(use(b, f"qt{g}").taken, use(b, f"qt{g}").after)
                if s_taken.due(b, n - 1):
                    pe.wait_ge(s_taken.sem, s_taken.at(b, n - 1))
                r = slice(j * HW, j * HW + RS)
                pe.matmul(psS[:, n % 2, :], chunk(Q1[r, g, :], c), KT[r, g, :],
                          start=True, stop=True).then_inc(s_full.sem, 1)

            def q2(b, g):
                pe.wait_ge(m_ready.sem, m_ready.at(b, g + 1))
                pe.wait_ge(use(b, f"q2_{g}").taken, use(b, f"q2_{g}").before)
                transposes(use(b, f"q2_{g}").bank, QA[:, :, g * G:(g + 1) * G, :].rearrange("p c h w -> p c (h w)")).then_inc(use(b, f"q2_{g}").full, 1)

            def score_t(b, post, g, c, j):
                n = g * NT * G + c * G + j
                if c == 0 and j == 0:
                    pe.wait_ge(use(b, f"q2_{g}").taken, use(b, f"q2_{g}").after)
                    if post is not None and h_taken.due(post, 2 * NF * g):
                        pe.wait_ge(h_taken.sem, h_taken.at(post, 2 * NF * g))
                if t_taken.due(b, n - 1):
                    pe.wait_ge(t_taken.sem, t_taken.at(b, n - 1))
                r = slice(j * HW, j * HW + RM)
                pe.matmul(psT[:, n % 2, :], chunk(KT[r, g, :], c), Q2[r, g % 2, :],
                          start=True, stop=True).then_inc(t_full.sem, 1)

            def times_v(b, g, c):
                pe.wait_ge(t_taken.sem, t_taken.at(b, g * NT * G + (c + 1) * G))
                if c == 0:
                    if cx_ready.due(b, g):
                        pe.wait_ge(cx_ready.sem, cx_ready.at(b, g))
                for j in range(G):
                    r = slice(j * HW, (j + 1) * HW)
                    last = pe.matmul(psV[r, :], VA[:, c, g * G + j, :], PT[:, (c % 2) * G + j, :],
                                     start=(c == 0), stop=(c == NT - 1))
                last.then_inc(v_full.sem, 1)

            def context(b, g):
                pe.wait_ge(ct_ready.sem, ct_ready.at(b, g + 1))
                for c in range(NT):
                    last = pe.transpose(chunk(psV, c), chunk(CT, c), ident[:, :])
                last.then_inc(c_full.sem, 1)

            def c_ctx(b):
                pe.wait_ge(cx_ready.sem, cx_ready.at(b, NG))
                pe.wait_ge(use(b, "ctx").taken, use(b, "ctx").before)
                transposes(use(b, "ctx").bank, CX[:, :, :, :].rearrange("p c h d -> p c (h d)")).then_inc(use(b, "ctx").full, 1)

            def c_out(b):
                pe.wait_ge(use(b, "ctx").taken, use(b, "ctx").after)
                pe.wait_ge(use(b, "out").taken, use(b, "out").before)
                to_tokens(use(b, "out").bank, CXT, sq["L0_ffn_Wo"][:, :]).then_inc(use(b, "out").full, 1)

            def c_norm(b):
                pe.wait_ge(use(b, "rows").taken, use(b, "rows").before)
                pe.wait_ge(zm_ready.sem, zm_ready.at(b, 1))
                transposes(use(b, "rows").bank, ZM).then_inc(use(b, "rows").full, 1)

            def c_logits(b):
                pe.wait_ge(use(b, "rows").taken, use(b, "rows").after)
                pe.wait_ge(use(b, "logits").taken, use(b, "logits").before)
                for c in range(NT):
                    last = pe.matmul(use(b, "logits").bank[:, c * E:(c + 1) * E], chunk(MT, c), wg[:, :], start=True, stop=True)
                last.then_inc(use(b, "logits").full, 1)

            def c_gate(b):
                pe.wait_ge(wt_ready.sem, wt_ready.at(b, 1))
                pe.wait_ge(use(b, "gate").taken, use(b, "gate").before)
                for c in range(NT):
                    last = pe.transpose(chunk(use(b, "gate").bank, c)[0:E, :], WT[:, c, :], ident[:, :])
                last.then_inc(use(b, "gate").full, 1)

            def c_bias(b):
                pe.wait_ge(use(b, "gate").taken, use(b, "gate").after)
                pe.wait_ge(use(b, "bias").taken, use(b, "bias").before)
                to_tokens(use(b, "bias").bank, WTT, b2[:, :]).then_inc(use(b, "bias").full, 1)

            def hidden(b, core, e, f):
                n = e * NF + f
                if n == 0:
                    pe.wait_ge(s_w1s, 1)
                if n % (2 * NF) == 0 and core is not None:
                    pe.wait_ge(t_taken.sem, t_taken.at(core, (n // (2 * NF) + 1) * NT * G))
                elif n > 1:
                    pe.wait_ge(h_taken.sem, h_taken.at(b, n - 1))
                w = slice(f * P, (f + 1) * P)
                bank = psT[:, f % 2, :]
                pe.matmul(bank, w1h[:, e, w], MH[:, :], start=True, stop=False)
                pe.matmul(bank, w1l[:, e, w], MH[:, :], start=False, stop=False)
                if n == 0:
                    pe.wait_ge(ml_ready.sem, ml_ready.at(b, 1))
                pe.matmul(bank, w1h[:, e, w], ML[:, :], start=False, stop=True).then_inc(h_full.sem, 1)

            def expert(b, e, c, f):
                if c == 0 and f == 0:
                    pe.wait_ge(s_w2, 16)
                    pe.wait_ge(h_taken.sem, h_taken.at(b, (e + 1) * NF))
                    pe.wait_ge(y_taken.sem, y_taken.at(b, e))
                last = pe.matmul(chunk(psY, c), chunk(H1[:, e % 2, f, :], c), w2[:, e, f, :],
                                 start=(f == 0), stop=(f == NF - 1))
                if c == NT - 1 and f == NF - 1:
                    last.then_inc(y_full.sem, 1)

            HEAD = {23: (head_rows,), 25: (head_k,), 25.5: (head_v,), 26: (head_r,)}
            TAIL = {9: (time_mix_out,), 10: (rows_1,), 12: (channel_mix_in(0),), 12.5: (channel_mix_in(1),),
                    14: (channel_mix_in(2),), 15: (channel_mix_in(3), receptance,), 16.5: (channel_mix,),
                    19: (rows_2,), 20: (project_k,), 21: (turn_k(0),), 22: (project_q,), 23: (turn_q(0),),
                    27: (turn_k(1),), 27.5: (turn_q(1),), 29.5: (project_v,)}
            CORE = {0.5: (turn_k(2),), 1: (turn_q(2),), 2: (turn_k(3),), 3: (turn_q(3),)}
            POST = {0: (c_out,), 2: (c_norm,), 3: (c_logits,), 11: (c_gate,), 13: (c_bias,)}

            def turn(*elements):
                for s, tail, head, core, post, past in roles(*elements):
                    g, k = divmod(s, PER)
                    nxt = core if g + 1 < NG else tail
                    tiles = score_tiles((g + 1) % NG, k) if nxt is not None else ()
                    now = (post, POST), (core, CORE), (head, HEAD), (tail, TAIL)
                    e, c = expert_chunk(s)
                    experts = past if s < FIRST else post
                    early, late = c == NT - 1, c == 0
                    if early and k >= NT and experts is not None:
                        for f in range(NF):
                            expert(experts, e, c, f)
                    extras(s, *now)
                    if k == 0 and not early and not late and experts is not None:
                        for f in range(NF):
                            expert(experts, e, c, f)
                    if k < NT:
                        for j in range(G):
                            if core is not None:
                                score_t(core, post, g, k, j)
                            if j >= G - len(tiles):
                                score(nxt, (g + 1) % NG, tiles[j - G + len(tiles)])
                            if not early and not late and experts is not None and k > 0:
                                expert(experts, e, c, j)
                            if (early and j < 2 or late and j >= 2) and experts is not None:
                                expert(experts, e, c, j % 2 * 2)
                                expert(experts, e, c, j % 2 * 2 + 1)
                            if k and j == 1 and core is not None:
                                times_v(core, g, k - 1)
                            if j == 1:
                                extras(s + 0.5, *now)
                    else:
                        for u in tiles[:len(tiles) // 2]:
                            score(nxt, (g + 1) % NG, u)
                        if k == NT and core is not None:
                            times_v(core, g, NT - 1)
                        if k == 5 and nxt is not None:
                            q2(nxt, (g + 1) % NG)
                        if post is not None:
                            hidden(post, core, 2 * g + (k - NT) // 2, (k - NT) % 2 * 2)
                        if not early and not late and experts is not None:
                            for f in range(NF):
                                expert(experts, e, c, f)
                        for u in tiles[len(tiles) // 2:]:
                            score(nxt, (g + 1) % NG, u)
                        extras(s + 0.5, *now)
                        if post is not None:
                            hidden(post, core, 2 * g + (k - NT) // 2, (k - NT) % 2 * 2 + 1)
                        if k == 5 and core is not None:
                            context(core, g)
                    if late and k >= NT and experts is not None:
                        for f in range(NF):
                            expert(experts, e, c, f)
                    if s == SLOTS - 1 and core is not None:
                        c_ctx(core)

            over(pe, turn)

        @block.vector
        def _(dve):
            own_h = Chain(dve, dve_h, 3)
            own_a = Chain(dve, dve_a, 8)
            own_m = Chain(dve, dve_m, NG)
            own_x = Chain(dve, dve_x, NG)
            own_c = Chain(dve, dve_c, 13)
            dve.wait_ge(s_dec, 1)
            dve.tensor_scalar(wdec[:, :], wdec[:, :], -1.0, None, ALU.mult).then_inc(s_wrow, 1)
            dve.memset(wrow[:, :], 0.0).then_inc(s_wrow, 1)
            dve.wait_ge(s_wrow, 2)
            dve.tensor_scalar(wrow[:, :], wrow[:, :], wdec[:, 0:1], None, ALU.add).then_inc(s_wrow, 1)
            dve.wait_ge(s_wrow, 3)
            dve.wait_ge(s_const, N_CONST)
            dve.tensor_copy(idle_dve[:, :], half[:, 0:1]).then_inc(y_taken.sem, 1)

            def split_w1():
                dve.wait_ge(s_w1, 16)
                dve.tensor_copy(w1h[:, :, :], w1).then_inc(s_wrow, 1)
                dve.wait_ge(s_wrow, 4)
                dve.tensor_tensor(w1l[:, :, :], w1, w1h[:, :, :].bitcast(F32), ALU.subtract).then_inc(s_w1s, 1)

            def stats(own, src, st, mv):
                for c in range(NT):
                    last = dve.bn_stats(st[:, c, :], src[:, c, :])
                own.step(last)
                own.wait()
                apart(dve)
                for c in range(NT):
                    last = dve.bn_aggr(mv[:, c, :], st[:, c, :])
                return last

            def normed(dst, src, mv, rs):
                for c in range(NT):
                    last = dve.tensor_scalar(dst[:, c, :], src[:, c, :], mv[:, c, 0:1], rs[:, c:c + 1],
                                             ALU.subtract, ALU.mult)
                return last

            def mix(dst, name):
                return dve.scalar_tensor_tensor(out=dst[:, :], in0=D[:, :], scalar=col[name], in1=XA[:, 0:T],
                                                op0=ALU.mult, op1=ALU.add)

            def head_stats(b):
                own_h.begin(b)
                dve.wait_ge(x_in.sem, x_in.at(b, 16))
                stats(own_h, X, stH, mvH).then_inc(h_stats.sem, 1)

            def head_norm(b):
                dve.wait_ge(h_rstd.sem, h_rstd.at(b, 1))
                normed(ZA, X, mvH, rsH[:, 3, :]).then_inc(zh_ready.sem, 1)
                normed(Z0, X, mvH, rsH[:, 0, :])

            def head_mixes(b):
                dve.wait_ge(hd_ready.sem, hd_ready.at(b, 1))
                for m, n in ((MK, "L0_attn_tm_k"), (MV, "L0_attn_tm_v"), (MR, "L0_attn_tm_r")):
                    mix(m, n).then_inc(hmix_ready.sem, 1)

            def wkv_args(b):
                dve.wait_ge(use(b, "K").taken, use(b, "K").after)
                own_h.link(dve.tensor_tensor_scan(PP[:, 1:T + 1], wrow[:, :], K[:, :], NEG, ALU.add, ALU.max))
                dve.scalar_tensor_tensor(out=EE[:, 0, :], in0=PP[:, 0:T], scalar=wdec[:, 0:1], in1=PP[:, 1:T + 1],
                                         op0=ALU.add, op1=ALU.subtract)
                dve.tensor_tensor(EE[:, 1, :], K[:, :], PP[:, 1:T + 1], ALU.subtract)
                own_h.link(dve.scalar_tensor_tensor(out=DD[:, :], in0=K[:, :], scalar=col["L0_attn_time_first"],
                                                    in1=PP[:, 0:T], op0=ALU.add, op1=ALU.subtract))
                dve.tensor_scalar(EE[:, 2, :], DD[:, :], 0.0, -1.0, ALU.max, ALU.mult)
                dve.tensor_scalar(EE[:, 3, :], DD[:, :], 0.0, None, ALU.min).then_inc(args_ready.sem, 1)
                own_h.end()

            def wkv_bb(b):
                dve.wait_ge(exps_ready.sem, exps_ready.at(b, 1))
                dve.tensor_tensor_scan(BB[:, 1:T + 1], EE[:, 0, :], EE[:, 1, :], 0.0, ALU.mult, ALU.add).then_inc(bb_ready.sem, 1)

            def wkv_ev(b):
                own_a.begin(b)
                dve.wait_ge(use(b, "V").taken, use(b, "V").after)
                own_a.step(dve.tensor_tensor(EV[:, :], EE[:, 1, :], V[:, :], ALU.mult))

            def wkv_aa(b):
                own_a.begin(b, 1)
                own_a.wait()
                own_a.step(dve.tensor_tensor_scan(AA[:, 1:T + 1], EE[:, 0, :], EV[:, :], 0.0, ALU.mult, ALU.add))

            def wkv_out(b):
                own_a.begin(b, 2)
                own_a.wait()
                own_a.step(dve.tensor_tensor(N1[:, :], EE[:, 2, :], AA[:, 0:T], ALU.mult))
                dve.wait_ge(d1_ready.sem, d1_ready.at(b, 1))
                own_a.link(dve.reciprocal(D1[:, :], D1[:, :]))
                dve.wait_ge(n2_ready.sem, n2_ready.at(b, 1))
                own_a.link(dve.tensor_tensor(N1[:, :], N1[:, :], N2[:, :], ALU.add))
                dve.wait_ge(r_ready.sem, r_ready.at(b, 1))
                own_a.link(dve.tensor_tensor(N1[:, :], N1[:, :], R[:, :], ALU.mult))
                dve.tensor_tensor(GT[:, :], N1[:, :], D1[:, :], ALU.mult).then_inc(g_ready.sem, 1)

            def stats_1(b):
                own_a.begin(b, 6)
                dve.wait_ge(use(b, "wo").full, use(b, "wo").after)
                dve.tensor_tensor(Y1[:, :, :], tokens(use(b, "wo").bank), Z0[:, :, :], ALU.add).then_inc(use(b, "wo").taken, 1)
                dve.wait_ge(use(b, "wo").taken, use(b, "wo").after)
                stats(own_a, Y1, stA, mvA).then_inc(a_stats.sem, 1)

            def norm_1(b):
                dve.wait_ge(a_rstd.sem, a_rstd.at(b, 1))
                normed(ZA, Y1, mvA, rsA[:, 0, :]).then_inc(za_ready.sem, 1)

            def mixes(b):
                dve.wait_ge(d_ready.sem, d_ready.at(b, 1))
                for m, n in ((MK, "L0_attn_cm_k"), (MR, "L0_attn_cm_r")):
                    mix(m, n).then_inc(mix_ready.sem, 1)

            def stats_2(b):
                own_a.begin(b, 7)
                dve.wait_ge(rt_ready.sem, rt_ready.at(b, 1))
                dve.wait_ge(use(b, "kv").full, use(b, "kv").after)
                dve.tensor_tensor(RT[:, :, :], tokens(use(b, "kv").bank), RT[:, :, :], ALU.mult).then_inc(use(b, "kv").taken, 1)
                dve.wait_ge(y1x_ready.sem, y1x_ready.at(b, 1))
                dve.wait_ge(use(b, "kv").taken, use(b, "kv").after)
                if kept.due(b, 0):
                    dve.wait_ge(kept.sem, kept.at(b, 0))
                dve.tensor_tensor(X1[:, :, :], RT[:, :, :], Y1[:, :, :], ALU.add).then_inc(x_used.sem, 1)
                dve.wait_ge(x_used.sem, x_used.at(b, 1))
                stats(own_a, X1, stA, mvA).then_inc(a_stats.sem, 1)
                own_a.end()

            def norm_2(b):
                dve.wait_ge(a_rstd.sem, a_rstd.at(b, 2))
                normed(ZA, X1, mvA, rsA[:, 3, :]).then_inc(za_ready.sem, 1)

            def split_k(b):
                dve.wait_ge(hi_ready.sem, hi_ready.at(b, 1))
                dve.tensor_tensor(KA[:, :, :, DH:2 * DH], heads(use(b, "k").bank), KA[:, :, :, 0:DH],
                                  ALU.subtract).then_inc(use(b, "k").taken, 1)

            def split_q(b):
                dve.wait_ge(hi_ready.sem, hi_ready.at(b, 2))
                dve.tensor_tensor(QA[:, :, :, 2 * DH:RS], heads(use(b, "q").bank), QA[:, :, :, 0:DH],
                                  ALU.subtract).then_inc(use(b, "q").taken, 1)

            def maximum(b, g, u):
                c, j = divmod(u, G)
                n = g * NT * G + u
                dve.wait_ge(s_full.sem, s_full.at(b, n + 1))
                dve.tensor_reduce(NM[:, c, g * G + j:g * G + j + 1], psS[:, n % 2, :], AX_X, ALU.max,
                                  negate=True).then_inc(s_taken.sem, 1)

            def maxima_beside_q(b, g):
                own_m.begin(b, g)
                dve.wait_ge(s_taken.sem, s_taken.at(b, (g + 1) * NT * G))
                hs = slice(g * G, (g + 1) * G)
                own_m.link(dve.tensor_copy(QA[:, :, hs, RS].bitcast(F32R), NM[:, :, hs]))
                dve.tensor_tensor(QA[:, :, hs, RS + 1], NM[:, :, hs], QA[:, :, hs, RS],
                                  ALU.subtract).then_inc(m_ready.sem, 1)

            def context_t(b, g):
                dve.wait_ge(v_full.sem, v_full.at(b, (g + 1) * NT))
                dve.tensor_copy(CT[:, :], psV[:, :]).then_inc(ct_ready.sem, 1)

            def context(b, g):
                dve.wait_ge(c_full.sem, c_full.at(b, g + 1))
                if g == 0:
                    own_x.begin(b)
                    if not isinstance(b, int) or b > 0:
                        dve.wait_ge(use(b - 1, "ctx").full, use(b - 1, "ctx").after)
                ctx4 = psV[:, :].rearrange("p (c j w) -> p c j w", c=NT, w=HW)
                own_x.link(dve.reciprocal(RD[:, :, :], ctx4[:, :, :, DH]))
                dve.tensor_tensor(CX[:, :, g * G:(g + 1) * G, :], ctx4[:, :, :, 0:DH],
                                  RD[:, :, :].unsqueeze(3).to_broadcast([P, NT, G, DH]), ALU.mult).then_inc(cx_ready.sem, 1)
                if g == NG - 1:
                    own_x.end()

            def c_ctx(b):
                own_c.begin(b)
                dve.wait_ge(kept.sem, kept.at(b, 1))
                dve.wait_ge(use(b, "out").full, use(b, "out").after)
                dve.tensor_tensor(XZ[:, :, :], tokens(use(b, "out").bank), XZ[:, :, :], ALU.add)
                dve.tensor_tensor(Y3[:, :, :], tokens(use(b, "out").bank), Z1b[:, :, :], ALU.add).then_inc(use(b, "out").taken, 1)
                dve.wait_ge(use(b, "out").taken, use(b, "out").after)
                stats(own_c, Y3, stC, mvC).then_inc(c_stats.sem, 1)

            def c_norm(b):
                dve.wait_ge(c_rstd.sem, c_rstd.at(b, 1))
                normed(ZM, Y3, mvC, rsC[:, 0, :]).then_inc(zm_ready.sem, 1)

            def bc(v):
                return v.unsqueeze(2).to_broadcast([P, NT, E])

            def c_gate(b):
                own_c.begin(b, 1)
                dve.wait_ge(use(b, "logits").full, use(b, "logits").after)
                logits = use(b, "logits").bank[:, 0:NT * E].rearrange("p (c e) -> p c e", e=E)
                own_c.link(dve.tensor_reduce(g1[:, :], logits, AX_X, ALU.max))
                dve.tensor_tensor(EX[:, :, :], logits, bc(g1[:, :]), ALU.subtract).then_inc(use(b, "logits").taken, 1)

            def c_top(b):
                own_c.begin(b, 2)
                dve.wait_ge(ex_ready.sem, ex_ready.at(b, 1))
                own_c.link(dve.tensor_reduce(g1[:, :], EX[:, :, :], AX_X, ALU.add))
                own_c.link(dve.reciprocal(g2[:, :], g1[:, :]))
                own_c.step(dve.tensor_tensor(PR[:, :, :], EX[:, :, :], bc(g2[:, :]), ALU.mult))
                own_c.wait()
                apart(dve)
                for c in range(NT):
                    last = dve.max(M8[:, c, :], PR[:, c, :])
                own_c.step(last)
                own_c.wait()
                apart(dve)
                for c in range(NT):
                    last = dve.max_index(I8[:, c, :], M8[:, c, :], PR[:, c, :])
                own_c.link(last)
                own_c.link(dve.tensor_copy(IF[:, :, :], I8[:, :, 0:2]))
                experts = iota[:, :].unsqueeze(1).to_broadcast([P, NT, E])
                dve.tensor_tensor(K0[:, :, :], experts, bc(IF[:, :, 0]), ALU.is_equal)
                own_c.link(dve.tensor_tensor(K1[:, :, :], experts, bc(IF[:, :, 1]), ALU.is_equal))
                own_c.link(dve.tensor_tensor(K0[:, :, :], K0[:, :, :], K1[:, :, :], ALU.add))
                own_c.link(dve.tensor_tensor(K1[:, :, :], PR[:, :, :], K0[:, :, :], ALU.mult))
                own_c.link(dve.tensor_reduce(g1[:, :], K1[:, :, :], AX_X, ALU.add))
                own_c.link(dve.reciprocal(g2[:, :], g1[:, :]))
                dve.tensor_tensor(WT[:, :, :], K1[:, :, :], bc(g2[:, :]), ALU.mult).then_inc(wt_ready.sem, 1)
                own_c.end()

            def c_bias(b):
                dve.wait_ge(use(b, "bias").full, use(b, "bias").after)
                dve.wait_ge(y_taken.sem, y_taken.at(b, 2))
                dve.tensor_tensor(RES[:, :, :], tokens(use(b, "bias").bank), RES[:, :, :], ALU.add).then_inc(use(b, "bias").taken, 1)

            def add_expert(b, e):
                dve.wait_ge(y_full.sem, y_full.at(b, e + 1))
                if e == 0:
                    dve.wait_ge(wt_ready.sem, wt_ready.at(b, 1))
                    dve.wait_ge(out_done.sem, out_done.at(b, 0))
                elif e == 2:
                    dve.wait_ge(use(b, "bias").taken, use(b, "bias").after)
                else:
                    dve.wait_ge(y_taken.sem, y_taken.at(b, e))
                before = XZ if e == 0 else RES
                for c in range(NT):
                    last = dve.scalar_tensor_tensor(out=RES[:, c, :], in0=chunk(psY, c), scalar=WT[:, c, e:e + 1],
                                                    in1=before[:, c, :], op0=ALU.mult, op1=ALU.add)
                last.then_inc(y_taken.sem, 1)

            HEAD = {20: (head_stats,), 21.5: (head_norm,), 24: (head_mixes,), 29: (wkv_args,)}
            TAIL = {2: (wkv_bb,), 2.5: (wkv_ev,), 3.5: (wkv_aa,), 5: (wkv_out,), 8.5: (stats_1,), 9.5: (norm_1,),
                    11.5: (mixes,), 16.5: (stats_2,), 18: (norm_2,), 20.5: (split_k,), 22: (split_q,)}
            POST = {0: (c_ctx,), 1.5: (c_norm,), 3: (c_gate,), 6.5: (c_top,), 14: (c_bias,)}

            def turn(*elements):
                for s, tail, head, core, post, past in roles(*elements):
                    g, k = divmod(s, PER)
                    nxt = core if g + 1 < NG else tail
                    tiles = score_tiles((g + 1) % NG, k) if nxt is not None else ()
                    now = (post, POST), (tail, TAIL), (head, HEAD)
                    e, c = expert_chunk(s)
                    experts = past if s < FIRST else post
                    if k == 5 and core is not None:
                        context_t(core, g)
                    if k == 5 and c == NT - 1 and experts is not None:
                        add_expert(experts, e)
                    extras(s, *now)
                    for u in tiles[:len(tiles) // 2]:
                        maximum(nxt, (g + 1) % NG, u)
                    if k < NT:
                        extras(s + 0.5, *now)
                    for u in tiles[len(tiles) // 2:]:
                        maximum(nxt, (g + 1) % NG, u)
                    if k == NT and nxt is not None:
                        maxima_beside_q(nxt, (g + 1) % NG)
                    if k == 6 and core is not None:
                        context(core, g)
                    if k >= NT:
                        extras(s + 0.5, *now)
                    if k == 1 and c == NT - 1 and experts is not None:
                        add_expert(experts, e)
                if elements[0] is None and elements[1] is not None:
                    split_w1()

            over(dve, turn)


_INS = VEC + SQUARE + ["L0_attn_x", "L0_attn_Wck", "L0_attn_Wcv", "L0_ffn_Wg", "L0_ffn_W1", "L0_ffn_b1",
                       "L0_ffn_W2", "L0_ffn_b2"]


def kernel(**inputs):
    import numpy as _np
    import concourse.bacc as _bacc
    from concourse import mybir as _mybir
    from concourse.bass_utils import run_bass_kernel_spmd as _run

    nc = _bacc.Bacc("TRN2", target_bir_lowering=False, num_devices=1)
    arrays, args = {}, {}
    for name in _INS:
        a = _np.ascontiguousarray(inputs[name])
        arrays[f"in_{name}_dram"] = a
        args[name] = nc.dram_tensor(f"in_{name}_dram", a.shape, _mybir.dt.from_np(a.dtype), kind="ExternalInput").ap()
    shape = inputs["L0_attn_x"].shape
    out = nc.dram_tensor("out_0_dram", shape, _mybir.dt.float32, kind="ExternalOutput").ap()
    build(nc, args, out)
    r = _run(nc, [arrays], core_ids=[0])
    return r.results[0]["out_0_dram"]
```
